# Optimizing a Trainium2 kernel written in Bass

```python
import numpy as np
import jax
import jax.numpy as jnp

def _softmax(x, axis=-1):
    return jax.nn.softmax(x, axis=axis)

def _gelu(x):
    return jax.nn.gelu(x, approximate=True)

def _silu(x):
    return jax.nn.silu(x)

def _sigmoid(x):
    return jax.nn.sigmoid(x)

def _layernorm(x, axis=-1, eps=1e-05):
    m = jnp.mean(x, axis=axis, keepdims=True)
    v = jnp.var(x, axis=axis, keepdims=True)
    return (x - m) / jnp.sqrt(v + eps)

def _scatter_add(tgt, idx, src, axis=0):
    return tgt.at[idx].add(src)

def _segment_sum(src, seg, n):
    return jax.ops.segment_sum(src, seg, n)
kernel_name = 'mk_xattn_ffn_d1_seqx_r8_990b0e'

def setup_inputs(seed: int=0):
    np.random.seed(seed)
    _w = jnp.asarray

    def _rec_inputs():
        import jax
        import jax.numpy as jnp
        _rk = jax.random.key(seed)
        x = 7.22e-05 + 1 * jax.random.normal(jax.random.fold_in(_rk, 1), (4, 256, 256), jnp.float32)
        _lenS = 256 - jax.random.randint(jax.random.fold_in(_rk, 7), (4,), 0, max(1, 256 // 4) + 1, jnp.int32)
        _lenS2 = 256 - jax.random.randint(jax.random.fold_in(_rk, 8), (4,), 0, max(1, 256 // 4) + 1, jnp.int32)
        _ctx_1024P = jax.random.normal(jax.random.fold_in(_rk, 11), (4, 16, 128), jnp.float32)
        _ctx_1024c = jax.random.dirichlet(jax.random.fold_in(_rk, 511), 0.3 * jnp.ones((16,), jnp.float32), (4, 256))
        _ctx_1024t = jnp.einsum('bsk,bkd->bsd', _ctx_1024c, _ctx_1024P)
        _ctx_1024t = _ctx_1024t * jax.lax.rsqrt(jnp.mean(jnp.square(_ctx_1024t)) + 1e-12) * 0.953939
        ctx_1024 = 2.81802e-05 + 1.00001 * (_ctx_1024t + 0.3 * jax.random.normal(jax.random.fold_in(_rk, 611), (4, 256, 128), jnp.float32))
        return (x, ctx_1024)
    x, ctx_1024 = _rec_inputs()

    def _L0_xattn_setup():
        import jax, jax.numpy as jnp
        import numpy as np
        key = jax.random.key(seed)
        ks = jax.random.split(key, 6)
        B, L, N, C, D = (8, 64, 256, 128, 128)
        return {'teacher_logits': jax.random.normal(ks[0], (B, L, N), dtype=jnp.float32), 'teacher_features': jax.random.normal(ks[1], (B, N, C), dtype=jnp.float32), 'Wq': jax.random.normal(ks[2], (D, C), dtype=jnp.float32) * (1.0 / np.sqrt(C)), 'bq': jnp.zeros((D,), dtype=jnp.float32), 'Wk': jax.random.normal(ks[3], (D, C), dtype=jnp.float32) * (1.0 / np.sqrt(C)), 'bk': jnp.zeros((D,), dtype=jnp.float32)}
    _L0_xattn_all = _L0_xattn_setup()
    _L0_xattn_in = {k: v for k, v in _L0_xattn_all.items() if k in ('Wq', 'bq', 'Wk', 'bk')}
    del _L0_xattn_all

    def _L0_ffn_setup():
        import jax, jax.numpy as jnp
        import numpy as np
        NUM_EXPERTS = 8
        TOP_K = 2
        MODEL_DIM = 256
        INTER_DIM = 128
        GATE_SCALE = 1.0
        UP_SCALE = 0.0
        key = jax.random.key(seed)
        k1, k2, k3, k4 = jax.random.split(key, 4)
        hidden_states = jax.random.normal(k1, (2, 256, MODEL_DIM), jnp.float32)
        router_gate = jax.random.normal(k2, (NUM_EXPERTS, MODEL_DIM), jnp.float32) * 0.02
        expert_gate_up = jax.random.normal(k3, (NUM_EXPERTS, MODEL_DIM, 2 * INTER_DIM), jnp.float32) * 0.02
        expert_down = jax.random.normal(k4, (NUM_EXPERTS, INTER_DIM, MODEL_DIM), jnp.float32) * 0.02
        return {'hidden_states': hidden_states, 'router_gate': router_gate, 'expert_gate_up': expert_gate_up, 'expert_down': expert_down}
    _L0_ffn_all = _L0_ffn_setup()
    _L0_ffn_in = {k: v for k, v in _L0_ffn_all.items() if k in ('router_gate', 'expert_gate_up', 'expert_down')}
    del _L0_ffn_all
    return {'x': x, 'ctx_1024': ctx_1024, 'L0_xattn_Wq': _L0_xattn_in['Wq'], 'L0_xattn_bq': _L0_xattn_in['bq'], 'L0_xattn_Wk': _L0_xattn_in['Wk'], 'L0_xattn_bk': _L0_xattn_in['bk'], 'L0_ffn_router_gate': _L0_ffn_in['router_gate'], 'L0_ffn_expert_gate_up': _L0_ffn_in['expert_gate_up'], 'L0_ffn_expert_down': _L0_ffn_in['expert_down']}

def reference(x, ctx_1024, L0_xattn_Wq, L0_xattn_bq, L0_xattn_Wk, L0_xattn_bk, L0_ffn_router_gate, L0_ffn_expert_gate_up, L0_ffn_expert_down):
    import jax
    import jax.numpy as jnp

    def _L0_xattn_ref(teacher_logits, teacher_features, Wq, bq, Wk, bk):
        import jax, jax.numpy as jnp
        import numpy as np
        query = jnp.einsum('bnc,dc->bnd', teacher_features, Wq) + bq
        key = jnp.einsum('bnc,dc->bnd', teacher_features, Wk) + bk
        energy = jnp.einsum('bnd,bmd->bnm', query, key)
        attention = jax.nn.softmax(energy, axis=-1)
        x_m = jnp.einsum('bln,bmn->blm', teacher_logits, attention)
        return x_m

    def _L0_ffn_ref(hidden_states, router_gate, expert_gate_up, expert_down):
        import jax, jax.numpy as jnp
        import numpy as np
        NUM_EXPERTS = 8
        TOP_K = 2
        MODEL_DIM = 256
        INTER_DIM = 128
        GATE_SCALE = 1.0
        UP_SCALE = 0.0
        orig_shape = hidden_states.shape
        hs = hidden_states.reshape(-1, orig_shape[-1])
        T = hs.shape[0]
        logits = hs @ router_gate.T
        probs = jax.nn.softmax(logits.astype(jnp.float32), axis=-1)
        topk_scores, topk_idx = jax.lax.top_k(probs, TOP_K)
        topk_scores = topk_scores / jnp.sum(topk_scores, axis=-1, keepdims=True)
        scores_f = topk_scores.T.reshape(-1).astype(hs.dtype)
        ids_f = topk_idx.T.reshape(-1)
        order = jnp.argsort(ids_f)
        sorted_ids = ids_f[order]
        scores_sorted = scores_f[order]
        token_slots = order % T
        x = hs[token_slots]
        inter = jnp.zeros((x.shape[0], 2 * INTER_DIM), x.dtype)
        for e in range(NUM_EXPERTS):
            m = (sorted_ids == e)[:, None]
            inter = inter + jnp.where(m, x, 0) @ expert_gate_up[e]
        gate = inter[..., 0::2]
        up = inter[..., 1::2]
        h = (up + UP_SCALE) * jax.nn.silu(gate * GATE_SCALE)
        out_rows = jnp.zeros((x.shape[0], MODEL_DIM), x.dtype)
        for e in range(NUM_EXPERTS):
            m = (sorted_ids == e)[:, None]
            out_rows = out_rows + jnp.where(m, h, 0) @ expert_down[e]
        out = jnp.zeros_like(hs).at[token_slots].add(out_rows * scores_sorted[:, None])
        return out.reshape(orig_shape)
    x = x + _L0_xattn_ref(_layernorm(x, axis=-1), ctx_1024, L0_xattn_Wq, L0_xattn_bq, L0_xattn_Wk, L0_xattn_bk)
    x = x + _L0_ffn_ref(_layernorm(x, axis=-1), L0_ffn_router_gate, L0_ffn_expert_gate_up, L0_ffn_expert_down)
    return x

_drawn_inputs = setup_inputs


def setup_inputs(seed=0):
    import zlib

    import numpy as np

    out = dict(_drawn_inputs(seed))
    spreads = {'L0_xattn_bq': (0.0, 0.1), 'L0_xattn_bk': (0.0, 0.8)}
    factors = {'L0_ffn_router_gate': 8.0, 'L0_ffn_expert_gate_up': 8.0, 'L0_ffn_expert_down': 8.0}
    for name, (base, spread) in spreads.items():
        noise = np.random.default_rng([zlib.crc32(name.encode()), seed]).standard_normal(out[name].shape)
        drawn = base * np.exp(spread * noise) if base else spread * noise
        out[name] = jnp.asarray(drawn.astype(out[name].dtype))
    for name, factor in factors.items():
        out[name] = (out[name] * factor).astype(out[name].dtype)
    return out
```

```python
import concourse.bass as bass
from concourse import mybir
from contextlib import ExitStack


def cross_attention_moe_kernel(
    nc: bass.Bass,
    x: bass.AP,
    ctx_feats: bass.AP,
    Wq: bass.AP,
    bq: bass.AP,
    Wk: bass.AP,
    bk: bass.AP,
    router_gate: bass.AP,
    gate_up: bass.AP,
    down: bass.AP,
    out: bass.AP,
):
    f32 = mybir.dt.float32
    f32r = mybir.dt.float32r
    ALU = mybir.AluOpType
    ACT = mybir.ActivationFunctionType
    AX = mybir.AxisListType

    P = 128
    B, L, N = x.shape
    D = Wq.shape[0]
    E = router_gate.shape[0]
    I = down.shape[1]
    EPS = 1e-5
    PAIRS = B // 2
    LT = L // P
    NT = N // P
    TP = 2 * LT
    TOK = 2 * L
    UNITS = PAIRS * E
    GU_LOADS = 4
    EL = E // GU_LOADS

    ctx = ExitStack()
    with ctx:
        def sb(name, shape, dt=f32):
            return ctx.enter_context(nc.sbuf_tensor(name, shape, dt))

        def sem(name):
            return ctx.enter_context(nc.semaphore(name))

        x_sb = sb("x_sb", [P, B * LT, N])
        x1_sb = sb("x1_sb", [P, B * LT, N])
        out_sb = sb("out_sb", [P, B * LT, N])
        ctx_sb = sb("ctx_sb", [P, B * NT, D])
        wqk_sb = sb("wqk_sb", [P, 2, D])
        bias_sb = sb("bias_sb", [P, 2])
        gate_sb = sb("gate_sb", [E, N])
        gu_raw = sb("gu_raw", [P, E, NT, 2 * I])
        down_raw = sb("down_raw", [P, E, N])
        gu_hi = sb("gu_hi", [P, E, NT, 2, I], f32r)
        gu_lo = sb("gu_lo", [P, E, NT, 2, I], f32r)
        down_hi = sb("down_hi", [P, E, N], f32r)
        down_lo = sb("down_lo", [P, E, N], f32r)
        ident = sb("ident", [P, P])
        minus_half = sb("minus_half", [P, TP])
        expert_no = sb("expert_no", [P, TP, E], mybir.dt.int32)
        expert_id = sb("expert_id", [P, TP, E])
        wqkT = sb("wqkT", [P, 2, P])
        gateT_hi = sb("gateT_hi", [P, NT, E], f32r)
        gateT_lo = sb("gateT_lo", [P, NT, E], f32r)
        ctxT = sb("ctxT", [P, 2 * N])
        qT = sb("qT", [P, 2 * N])
        kT = sb("kT", [P, 2 * N])
        stats = sb("stats", [P, TP, 6])
        mean_var = sb("mean_var", [P, TP, 2])
        var_eps = sb("var_eps", [P, TP])
        rstd = sb("rstd", [P, TP])
        ln = sb("ln", [P, TP, N])
        lnT = sb("lnT", [P, 2, NT, L])
        neg_max = sb("neg_max", [P, TP])
        probs = sb("probs", [P, TP, N])
        denom = sb("denom", [P, TP])
        rdenom = sb("rdenom", [P, TP])
        probsT = sb("probsT", [P, 2, NT, N])
        stats2 = sb("stats2", [P, TP, 6])
        mean_var2 = sb("mean_var2", [P, TP, 2])
        var_eps2 = sb("var_eps2", [P, TP])
        rstd2 = sb("rstd2", [P, TP])
        hs = sb("hs", [P, TP, N])
        hsT_hi = sb("hsT_hi", [P, PAIRS, NT, TOK], f32r)
        hsT_lo = sb("hsT_lo", [P, PAIRS, NT, TOK], f32r)
        logits = sb("logits", [P, TP, E])
        top = sb("top", [P, TP, 8])
        top_no = sb("top_no", [P, TP, 8], mybir.dt.uint32)
        top_id = sb("top_id", [P, TP, 2])
        gap = sb("gap", [P, TP])
        e_gap = sb("e_gap", [P, TP])
        one_e = sb("one_e", [P, TP])
        inv_e = sb("inv_e", [P, TP])
        w_top = sb("w_top", [P, TP, 2])
        is_top = sb("is_top", [P, 2, TP, E])
        w_is_top = sb("w_is_top", [P, 2, TP, E])
        scores = sb("scores", [P, TP, E])
        scoresT = sb("scoresT", [E, TOK])
        score_row = sb("score_row", [1, PAIRS, E, TOK])
        score_bc = sb("score_bc", [P, 2, TOK])
        tanh_g = sb("tanh_g", [P, 2, TOK])
        scaled = sb("scaled", [P, TOK])
        gated = sb("gated", [P, TOK])
        h = sb("h", [P, 2, TOK])
        h_hi = sb("h_hi", [P, 2, TOK], f32r)
        h_lo = sb("h_lo", [P, 2, TOK], f32r)

        def bank(name, shape):
            return ctx.enter_context(nc.psum_tensor(name, shape, f32))

        ps_g = [bank(f"ps_g{i}", [P, TOK]) for i in range(2)]
        ps_u = [bank(f"ps_u{i}", [P, TOK]) for i in range(2)]
        ps_out = [bank(f"ps_out{i}", [P, 2, N]) for i in range(2)]
        ps_a = [bank(f"ps_a{i}", [P, TOK]) for i in range(2)]

        x_in = [sem(f"x_in{p}") for p in range(PAIRS)]
        ctx_in = [sem(f"ctx_in{p}") for p in range(PAIRS)]
        wqk_in = sem("wqk_in")
        small_in = sem("small_in")
        gu_in = [sem(f"gu_in{i}") for i in range(GU_LOADS)]
        down_in = [sem(f"down_in{i}") for i in range(2)]
        consts = sem("consts")
        att_filled = sem("att_filled")
        act_drained = sem("act_drained")
        dve_drained = sem("dve_drained")
        dve_step = sem("dve_step")
        var_ready = sem("var_ready")
        rstd_ready = sem("rstd_ready")
        ln_ready = sem("ln_ready")
        max_ready = sem("max_ready")
        exp_ready = sem("exp_ready")
        probs_ready = sem("probs_ready")
        hi_ready = sem("hi_ready")
        gap_ready = sem("gap_ready")
        egap_ready = sem("egap_ready")
        scores_ready = sem("scores_ready")
        row_ready = sem("row_ready")
        gu_hi_ready = sem("gu_hi_ready")
        gu_lo_ready = sem("gu_lo_ready")
        down_hi_ready = sem("down_hi_ready")
        down_lo_ready = sem("down_lo_ready")
        gu_filled = sem("gu_filled")
        tanh_ready = sem("tanh_ready")
        bc_ready = sem("bc_ready")
        scaled_ready = sem("scaled_ready")
        gated_ready = sem("gated_ready")
        h_ready = sem("h_ready")
        h_hi_ready = sem("h_hi_ready")
        h_lo_ready = sem("h_lo_ready")
        down_done = sem("down_done")
        out_ps0_ready = sem("out_ps0_ready")
        out_ready = sem("out_ready")
        stored = [sem(f"stored{b}") for b in range(B)]

        USES = [("ctxT", "act"), ("q", "act"), ("k", "dve"), ("E0", "act"), ("E1", "act"),
                ("LT0", "dve"), ("LT1", "dve"), ("AT0", "act"), ("AT1", "act"),
                ("M0", "dve"), ("M1", "dve"), ("H0", "dve"), ("H1", "dve"),
                ("logits", "dve"), ("scoresT", "act")]
        NAMES = [n for n, _ in USES]
        FILL0 = 2
        DRAIN0 = 1
        WIDE = [ps_g[0], ps_a[0], ps_a[1], ps_u[0], ps_g[1], ps_u[1]]

        def bank_of(p, name):
            k = NAMES.index(name)
            return WIDE[k % 6] if p == 0 else ps_a[k % 2]

        def filled(p, name):
            return FILL0 + p * len(USES) + NAMES.index(name) + 1

        def drain_count(p, name):
            who = USES[NAMES.index(name)][1]
            per = sum(w == who for _, w in USES)
            return DRAIN0 + p * per + sum(w == who for _, w in USES[:NAMES.index(name) + 1])

        def wait_drained(eng, p, name):
            who = USES[NAMES.index(name)][1]
            eng.wait_ge(act_drained if who == "act" else dve_drained, drain_count(p, name))

        WOVEN = [[["scoresT"], ["ctxT"]], [["q", "k"], ["E0"]], [["E1"], ["LT0"]],
                 [["LT1"], ["AT0"]], [["AT1"], ["M0"]], [["M1"], ["H0"]],
                 [["H1"], ["logits"]], [[], ["scoresT"]]]

        def woven(U, slot, stage):
            if U < E:
                for name in WOVEN[U][slot]:
                    stage(0 if U == 0 and slot == 0 else 1, name)

        def gu_src(e):
            return gu_raw[:, e].rearrange("p k (i two) -> p k two i", two=2)

        block = ctx.enter_context(nc.Block())

        @block.sync
        def _(sp):
            def load_x(p):
                sp.dma_start(x_sb[:, p * TP:(p + 1) * TP, :],
                             x[2 * p:2 * p + 2].rearrange("b (t q) n -> q (b t) n", q=P)).then_inc(x_in[p], 16)

            load_x(0)
            sp.dma_start(gate_sb[:], router_gate).then_inc(small_in, 16)
            for i in range(GU_LOADS):
                es = slice(i * EL, (i + 1) * EL)
                sp.dma_start(gu_raw[:, es], gate_up[es].rearrange("e (k q) f -> q e k f", q=P)).then_inc(gu_in[i], 16)
                if i == 1:
                    load_x(1)
            for p in range(PAIRS):
                wait_drained(sp, p, "scoresT")
                sp.dma_start(score_row[0:1, p], scoresT[:]).then_inc(row_ready, 16)
            for b in range(B):
                sp.wait_ge(out_ready, b + 1)
                sp.dma_start(out[b].rearrange("(t q) n -> q t n", q=P),
                             out_sb[:, b * LT:(b + 1) * LT, :]).then_inc(stored[b], 16)
            for b in range(B):
                sp.wait_ge(stored[b], 16)

        @block.gpsimd
        def _(pool):
            nc.gpsimd.memset(ident[:], 0.0).then_inc(consts, 1)
            nc.gpsimd.memset(minus_half[:], -0.5).then_inc(consts, 1)
            pool.wait_ge(consts, 1)
            nc.gpsimd.affine_select(out=ident[:], in_=ident[:], compare_op=ALU.not_equal, fill=1.0, base=0,
                                    pattern=[[-1, P]], channel_multiplier=1).then_inc(consts, 1)
            nc.gpsimd.iota(expert_no[:], pattern=[[0, TP], [1, E]], base=0, channel_multiplier=0).then_inc(consts, 1)

            def inv_sqrt(n, src, dst):
                pool.wait_ge(var_ready, n)
                nc.gpsimd.tensor_tensor(dst[:], src[:], minus_half[:], ALU.pow).then_inc(rstd_ready, 1)

            def inv_sqrt_batch(n, bi):
                pool.wait_ge(var_ready, n)
                t = slice(bi * LT, (bi + 1) * LT)
                nc.gpsimd.tensor_tensor(rstd2[:, t], var_eps2[:, t], minus_half[:, t], ALU.pow).then_inc(rstd_ready, 1)

            def gu_lo_part(e):
                pool.wait_ge(gu_hi_ready, e + 1)
                nc.gpsimd.tensor_tensor(gu_lo[:, e], gu_src(e), gu_hi[:, e].bitcast(f32),
                                        ALU.subtract).then_inc(gu_lo_ready, 1)

            def down_lo_part(e):
                pool.wait_ge(down_hi_ready, e + 1)
                nc.gpsimd.tensor_tensor(down_lo[:, e], down_raw[:, e], down_hi[:, e].bitcast(f32),
                                        ALU.subtract).then_inc(down_lo_ready, 1)

            def broadcast(U):
                p, e = divmod(U, E)
                if e == 0:
                    pool.wait_ge(row_ready, 16 * (p + 1))
                if U >= 2:
                    pool.wait_ge(scaled_ready, U - 1)
                nc.gpsimd.partition_broadcast(score_bc[:, U % 2], score_row[0:1, p, e], P).then_inc(bc_ready, 1)

            inv_sqrt(1, var_eps, rstd)
            for e in range(4):
                gu_lo_part(e)
            inv_sqrt_batch(2, 0)
            inv_sqrt_batch(3, 1)
            for e in range(4, E):
                gu_lo_part(e)
            down_lo_part(0)
            broadcast(0)
            for U in range(UNITS):
                if U + 1 < UNITS and U + 1 != E:
                    broadcast(U + 1)
                if U + 1 < E:
                    down_lo_part(U + 1)
                if U == 0:
                    inv_sqrt(4, var_eps, rstd)
                if U == 5:
                    inv_sqrt_batch(5, 0)
                if U == 6:
                    inv_sqrt_batch(6, 1)
                if U + 1 == E:
                    broadcast(U + 1)
                pool.wait_ge(h_hi_ready, U + 1)
                if U >= 2:
                    pool.wait_ge(down_done, U - 1)
                nc.gpsimd.tensor_tensor(h_lo[:, U % 2], h[:, U % 2], h_hi[:, U % 2].bitcast(f32),
                                        ALU.subtract).then_inc(h_lo_ready, 1)

        @block.tensor
        def _(pe):
            def att(p, name):
                k = NAMES.index(name)
                ring = 6 if p == 0 else 2
                if k >= ring:
                    wait_drained(pe, p, NAMES[k - ring])
                elif p == 1:
                    wait_drained(pe, 0, "scoresT")
                    wait_drained(pe, 0, "logits")
                dst = bank_of(p, name)
                if name == "ctxT":
                    pe.wait_ge(ctx_in[p], 16)
                    for j in range(TP):
                        last = nc.tensor.transpose(dst[:, j * P:(j + 1) * P], ctx_sb[:, p * TP + j], ident[:])
                elif name in ("q", "k"):
                    wait_drained(pe, p, "ctxT")
                    last = nc.tensor.matmul(dst[:], wqkT[:, "qk".index(name)], ctxT[:], start=True, stop=True)
                elif name[0] == "E":
                    wait_drained(pe, p, "q")
                    wait_drained(pe, p, "k")
                    o = int(name[1]) * N
                    for t in range(NT):
                        last = nc.tensor.matmul(dst[:, t * N:(t + 1) * N], qT[:, o + t * P:o + (t + 1) * P],
                                                kT[:, o:o + N], start=True, stop=True)
                elif name[:2] in ("LT", "AT"):
                    bi = int(name[2])
                    if name[0] == "L":
                        src = ln
                        pe.wait_ge(ln_ready, p * 2 * TP + (bi + 1) * LT)
                    else:
                        src = probs
                        pe.wait_ge(probs_ready, 2 * p + bi + 1)
                    v = dst[:].rearrange("q (k r) -> q k r", k=NT)
                    for t in range(2):
                        for c in range(NT):
                            last = nc.tensor.transpose(v[:, c, t * P:(t + 1) * P],
                                                       src[:, bi * LT + t, c * P:(c + 1) * P], ident[:])
                elif name[0] == "M":
                    bi = int(name[1])
                    wait_drained(pe, p, f"LT{bi}")
                    wait_drained(pe, p, f"AT{bi}")
                    for t in range(LT):
                        for c in range(NT):
                            last = nc.tensor.matmul(dst[:, t * N:(t + 1) * N], lnT[:, bi, c, t * P:(t + 1) * P],
                                                    probsT[:, bi, c], start=(c == 0), stop=(c == NT - 1))
                elif name[0] == "H":
                    bi = int(name[1])
                    pe.wait_ge(ln_ready, p * 2 * TP + TP + (bi + 1) * LT)
                    v = dst[:].rearrange("q (k r) -> q k r", k=NT)
                    for t in range(LT):
                        for c in range(NT):
                            last = nc.tensor.transpose(v[:, c, t * P:(t + 1) * P],
                                                       hs[:, bi * LT + t, c * P:(c + 1) * P], ident[:])
                elif name == "logits":
                    wait_drained(pe, p, "H1")
                    for j in range(TP):
                        cols = slice(j * P, (j + 1) * P)
                        terms = [(a, g, c) for a, g in ((hsT_lo, gateT_hi), (hsT_hi, gateT_lo), (hsT_hi, gateT_hi))
                                 for c in range(NT)]
                        for i, (a, g, c) in enumerate(terms):
                            last = nc.tensor.matmul(dst[:, j * E:(j + 1) * E], a[:, p, c, cols], g[:, c],
                                                    start=(i == 0), stop=(i == len(terms) - 1))
                else:
                    pe.wait_ge(scores_ready, p + 1)
                    for j in range(TP):
                        last = nc.tensor.transpose(dst[0:E, j * P:(j + 1) * P], scores[:, j], ident[:])
                last.then_inc(att_filled, 1)

            pe.wait_ge(consts, 4)
            pe.wait_ge(wqk_in, 32)
            for i in range(2):
                last = nc.tensor.transpose(ps_a[0][:, i * P:(i + 1) * P], wqk_sb[:, i], ident[:])
            last.then_inc(att_filled, 1)
            pe.wait_ge(small_in, 16 * 3)
            for c in range(NT):
                last = nc.tensor.transpose(ps_a[1][:, c * E:(c + 1) * E], gate_sb[:, c * P:(c + 1) * P],
                                           ident[0:E, 0:E])
            last.then_inc(att_filled, 1)
            pe.wait_ge(act_drained, DRAIN0)
            pe.wait_ge(dve_drained, DRAIN0)
            for name in NAMES[:-1]:
                att(0, name)

            def gate_up_unit(U):
                p, e = divmod(U, E)
                if e == 0:
                    wait_drained(pe, p, "H1")
                if p == 0:
                    pe.wait_ge(gu_lo_ready, e + 1)
                if U >= 2:
                    pe.wait_ge(h_ready, U - 1)
                terms = [(w, a, c) for w, a in ((gu_lo, hsT_hi), (gu_hi, hsT_lo), (gu_hi, hsT_hi)) for c in range(NT)]
                for half, dst in enumerate((ps_g[U % 2], ps_u[U % 2])):
                    for i, (w, a, c) in enumerate(terms):
                        last = nc.tensor.matmul(dst[:], w[:, e, c, half], a[:, p, c],
                                                start=(i == 0), stop=(i == len(terms) - 1))
                    last.then_inc(gu_filled, 1)

            def down_unit(U):
                p, e = divmod(U, E)
                pe.wait_ge(h_lo_ready, U + 1)
                if p == 0:
                    pe.wait_ge(down_lo_ready, e + 1)
                if e == 0 and p > 0:
                    pe.wait_ge(out_ready, 2 * p)
                for j in range(TP):
                    cols = slice(j * P, (j + 1) * P)
                    dst = ps_out[j // 2][:, j % 2]
                    terms = ((h_lo, down_hi), (h_hi, down_lo), (h_hi, down_hi))
                    for i, (a, w) in enumerate(terms):
                        last = nc.tensor.matmul(dst, a[:, U % 2, cols], w[:, e],
                                                start=(e == 0 and i == 0 and j % 2 == 0),
                                                stop=(e == E - 1 and i == 2), skip_group_check=True)
                    if j == TP - 1:
                        last.then_inc(down_done, 1)
                    elif e == E - 1 and j % 2 == 1:
                        last.then_inc(out_ps0_ready, 1)

            for U in range(UNITS + 2):
                if U < UNITS:
                    gate_up_unit(U)
                woven(U, 0, att)
                if U >= 2:
                    down_unit(U - 2)
                woven(U, 1, att)

        @block.scalar
        def _(act):
            act.dma_start(ctx_sb[:, 0:TP], ctx_feats[0:2].rearrange("b (t q) d -> q (b t) d", q=P)).then_inc(ctx_in[0], 16)
            act.dma_start(wqk_sb[:, 0], Wq).then_inc(wqk_in, 16)
            act.dma_start(wqk_sb[:, 1], Wk).then_inc(wqk_in, 16)
            act.dma_start(bias_sb[:, 0:1], bq.rearrange("(d o) -> d o", o=1)).then_inc(small_in, 16)
            act.dma_start(bias_sb[:, 1:2], bk.rearrange("(d o) -> d o", o=1)).then_inc(small_in, 16)
            act.dma_start(ctx_sb[:, TP:], ctx_feats[2:4].rearrange("b (t q) d -> q (b t) d", q=P)).then_inc(ctx_in[1], 16)
            for i in range(2):
                es = slice(i * E // 2, (i + 1) * E // 2)
                act.dma_start(down_raw[:, es], down[es].rearrange("e i n -> i e n")).then_inc(down_in[i], 16)

            def att(p, name):
                if name in ("ctxT", "AT0", "AT1"):
                    src = bank_of(p, name)
                    act.wait_ge(att_filled, filled(p, name))
                    if name == "ctxT":
                        nc.scalar.copy(ctxT[:], src[:]).then_inc(act_drained, 1)
                    else:
                        nc.scalar.copy(probsT[:, int(name[2])].rearrange("q k r -> q (k r)"), src[:]).then_inc(act_drained, 1)
                elif name == "q":
                    act.wait_ge(att_filled, filled(p, name))
                    act.wait_ge(small_in, 16 * 3)
                    nc.scalar.activation(qT[:], bank_of(p, name)[:], ACT.Identity,
                                         bias=bias_sb[:, 0:1]).then_inc(act_drained, 1)
                elif name in ("E0", "E1"):
                    bi = int(name[1])
                    act.wait_ge(max_ready, 2 * p + bi + 1)
                    src = bank_of(p, name)
                    for t in range(2):
                        j = 2 * bi + t
                        nc.scalar.activation(probs[:, j], src[:, t * N:(t + 1) * N], ACT.Exp,
                                             bias=neg_max[:, j:j + 1],
                                             accum_out=denom[:, j:j + 1]).then_inc(exp_ready, 1)
                    act.wait_ge(exp_ready, 4 * p + 2 * bi + 2)
                    act.sem_inc(act_drained, 1)
                elif name in ("H0", "H1"):
                    bi = int(name[1])
                    act.wait_ge(att_filled, filled(p, name))
                    v = bank_of(p, name)[:].rearrange("q (k r) -> q k r", k=NT)
                    nc.scalar.copy(hsT_hi[:, p, :, bi * L:(bi + 1) * L], v).then_inc(hi_ready, 1)
                elif name == "logits":
                    act.wait_ge(gap_ready, p + 1)
                    nc.scalar.activation(e_gap[:], gap[:], ACT.Exp).then_inc(egap_ready, 1)
                elif name == "scoresT":
                    act.wait_ge(att_filled, filled(p, name))
                    if p > 0:
                        act.wait_ge(row_ready, 16 * p)
                    nc.scalar.copy(scoresT[:], bank_of(p, name)[0:E, :]).then_inc(act_drained, 1)

            act.wait_ge(att_filled, 1)
            nc.scalar.copy(wqkT[:].rearrange("q a b -> q (a b)"), ps_a[0][:, 0:2 * P]).then_inc(act_drained, 1)
            for name in NAMES[:-1]:
                att(0, name)
            for U in range(UNITS):
                act.wait_ge(gu_filled, 2 * U + 1)
                if U >= 2:
                    act.wait_ge(scaled_ready, U - 1)
                nc.scalar.activation(tanh_g[:, U % 2], ps_g[U % 2][:], ACT.Tanh, scale=0.5).then_inc(tanh_ready, 1)
                woven(U, 0, att)
                act.wait_ge(h_ready, U + 1)
                if U >= 2:
                    act.wait_ge(down_done, U - 1)
                nc.scalar.copy(h_hi[:, U % 2], h[:, U % 2]).then_inc(h_hi_ready, 1)
                woven(U, 1, att)

        @block.vector
        def _(dve):
            steps = [0]

            def step(ins):
                ins.then_inc(dve_step, 1)
                steps[0] += 1
                dve.wait_ge(dve_step, steps[0])

            def mean_and_var(src, tiles, st, mv, ve):
                for i, j in enumerate(tiles):
                    ins = nc.vector.bn_stats(st[:, j], src(j))
                    ins.then_inc(dve_step, 1)
                    steps[0] += 1
                dve.wait_ge(dve_step, steps[0])
                for j in tiles:
                    ins = nc.vector.bn_aggr(mv[:, j], st[:, j])
                    ins.then_inc(dve_step, 1)
                    steps[0] += 1
                dve.wait_ge(dve_step, steps[0])
                t = slice(tiles[0], tiles[-1] + 1)
                nc.vector.tensor_scalar_add(ve[:, t], mv[:, t, 1], EPS).then_inc(var_ready, 1)

            def normalise(n, src, tiles, mv, rs, dst):
                dve.wait_ge(rstd_ready, n)
                for j in tiles:
                    nc.vector.tensor_scalar(dst[:, j], src(j), mv[:, j, 0:1], rs[:, j:j + 1],
                                            ALU.subtract, ALU.mult).then_inc(ln_ready, 1)

            def att(p, name):
                def xt(j):
                    return x_sb[:, p * TP + j]

                def x1t(j):
                    return x1_sb[:, p * TP + j]

                if name == "ctxT":
                    dve.wait_ge(x_in[p], 16)
                    mean_and_var(xt, list(range(TP)), stats, mean_var, var_eps)
                elif name == "k":
                    dve.wait_ge(att_filled, filled(p, name))
                    dve.wait_ge(small_in, 16 * 3)
                    nc.vector.tensor_scalar(kT[:], bank_of(p, name)[:], bias_sb[:, 1:2], None,
                                            ALU.add).then_inc(dve_drained, 1)
                    normalise(3 * p + 1, xt, list(range(TP)), mean_var, rstd, ln)
                elif name in ("E0", "E1"):
                    bi = int(name[1])
                    dve.wait_ge(att_filled, filled(p, name))
                    nc.vector.tensor_reduce(neg_max[:, 2 * bi:2 * bi + 2],
                                            bank_of(p, name)[:].rearrange("q (t n) -> q t n", t=2),
                                            AX.X, ALU.max, negate=True).then_inc(max_ready, 1)
                elif name in ("LT0", "LT1"):
                    bi = int(name[2])
                    dve.wait_ge(att_filled, filled(p, name))
                    nc.vector.tensor_copy(lnT[:, bi].rearrange("q k r -> q (k r)"),
                                          bank_of(p, name)[:]).then_inc(dve_drained, 1)
                    dve.wait_ge(exp_ready, 4 * p + 2 * bi + 2)
                    step(nc.vector.reciprocal(rdenom[:, 2 * bi:2 * bi + 2], denom[:, 2 * bi:2 * bi + 2]))
                    for t in range(2):
                        j = 2 * bi + t
                        last = nc.vector.tensor_scalar(probs[:, j], probs[:, j], rdenom[:, j:j + 1], None, ALU.mult)
                    last.then_inc(probs_ready, 1)
                elif name in ("M0", "M1"):
                    bi = int(name[1])
                    t0 = p * TP + bi * LT
                    dve.wait_ge(att_filled, filled(p, name))
                    ins = nc.vector.tensor_tensor(x1_sb[:, t0:t0 + LT].rearrange("q t n -> q (t n)"),
                                                  bank_of(p, name)[:],
                                                  x_sb[:, t0:t0 + LT].rearrange("q t n -> q (t n)"), ALU.add)
                    ins.then_inc(dve_drained, 1)
                    dve.wait_ge(dve_drained, drain_count(p, name))
                    mean_and_var(x1t, [bi * LT, bi * LT + 1], stats2, mean_var2, var_eps2)
                elif name in ("H0", "H1"):
                    bi = int(name[1])
                    dve.wait_ge(hi_ready, 2 * p + bi + 1)
                    v = bank_of(p, name)[:].rearrange("q (k r) -> q k r", k=NT)
                    cols = slice(bi * L, (bi + 1) * L)
                    nc.vector.tensor_tensor(hsT_lo[:, p, :, cols], v, hsT_hi[:, p, :, cols].bitcast(f32),
                                            ALU.subtract).then_inc(dve_drained, 1)
                elif name == "logits":
                    route(p)

            def norm_x1(p, bi):
                normalise(3 * p + 2 + bi, lambda j: x1_sb[:, p * TP + j], [bi * LT, bi * LT + 1],
                          mean_var2, rstd2, hs)

            def route(p):
                dve.wait_ge(att_filled, filled(p, "logits"))
                ins = nc.vector.tensor_copy(logits[:].rearrange("q t e -> q (t e)"),
                                            bank_of(p, "logits")[:, 0:TP * E])
                ins.then_inc(dve_drained, 1)
                dve.wait_ge(dve_drained, drain_count(p, "logits"))
                for j in range(TP):
                    ins = nc.vector.max(top[:, j], logits[:, j])
                    ins.then_inc(dve_step, 1)
                    steps[0] += 1
                dve.wait_ge(dve_step, steps[0])
                nc.vector.tensor_tensor(gap[:], top[:, :, 1], top[:, :, 0], ALU.subtract).then_inc(gap_ready, 1)
                for j in range(TP):
                    ins = nc.vector.max_index(top_no[:, j], top[:, j], logits[:, j])
                    ins.then_inc(dve_step, 1)
                    steps[0] += 1
                dve.wait_ge(dve_step, steps[0])
                step(nc.vector.tensor_copy(top_id[:], top_no[:, :, 0:2]))
                for r in range(2):
                    ins = nc.vector.tensor_tensor(is_top[:, r], expert_id[:],
                                                  top_id[:, :, r:r + 1].broadcast_to([P, TP, E]), ALU.is_equal)
                    ins.then_inc(dve_step, 1)
                    steps[0] += 1
                dve.wait_ge(egap_ready, p + 1)
                step(nc.vector.tensor_scalar(one_e[:], e_gap[:], 1.0, 2.0, ALU.add, ALU.mult))
                step(nc.vector.reciprocal(w_top[:, :, 0], one_e[:]))
                step(nc.vector.tensor_tensor(w_top[:, :, 1], w_top[:, :, 0], e_gap[:], ALU.mult))
                for r in range(2):
                    ins = nc.vector.tensor_tensor(w_is_top[:, r], is_top[:, r],
                                                  w_top[:, :, r:r + 1].broadcast_to([P, TP, E]), ALU.mult)
                    ins.then_inc(dve_step, 1)
                    steps[0] += 1
                dve.wait_ge(dve_step, steps[0])
                nc.vector.tensor_tensor(scores[:], w_is_top[:, 0], w_is_top[:, 1], ALU.add).then_inc(scores_ready, 1)

            def split_gu(e):
                if e % EL == 0:
                    dve.wait_ge(gu_in[e // EL], 16)
                nc.vector.tensor_copy(gu_hi[:, e], gu_src(e)).then_inc(gu_hi_ready, 1)

            def split_down(e):
                if e % (E // 2) == 0:
                    dve.wait_ge(down_in[e // (E // 2)], 16)
                nc.vector.tensor_copy(down_hi[:, e], down_raw[:, e]).then_inc(down_hi_ready, 1)

            dve.wait_ge(consts, 4)
            step(nc.vector.tensor_copy(expert_id[:], expert_no[:]))
            dve.wait_ge(att_filled, 2)
            gate_ps = ps_a[1][:, 0:NT * E].rearrange("q (c e) -> q c e", c=NT)
            step(nc.vector.tensor_copy(gateT_hi[:], gate_ps))
            nc.vector.tensor_tensor(gateT_lo[:], gate_ps, gateT_hi[:].bitcast(f32), ALU.subtract).then_inc(dve_drained, 1)
            for name in ("ctxT", "q", "k", "E0", "E1"):
                att(0, name)
            for e in range(4):
                split_gu(e)
            for name in ("LT0", "LT1", "M0", "M1"):
                att(0, name)
            norm_x1(0, 0)
            norm_x1(0, 1)
            for e in range(4, E):
                split_gu(e)
            for name in ("H0", "H1", "logits"):
                att(0, name)
            for e in range(E):
                split_down(e)

            def finish(p, i):
                t0 = p * TP + i * LT
                if i == 0:
                    dve.wait_ge(out_ps0_ready, p + 1)
                else:
                    dve.wait_ge(down_done, (p + 1) * E)
                nc.vector.tensor_tensor(out_sb[:, t0:t0 + LT], ps_out[i][:], x1_sb[:, t0:t0 + LT],
                                        ALU.add).then_inc(out_ready, 1)

            for U in range(UNITS):
                dve.wait_ge(tanh_ready, U + 1)
                dve.wait_ge(bc_ready, U + 1)
                nc.vector.scalar_tensor_tensor(out=scaled[:], in0=tanh_g[:, U % 2], scalar=1.0, in1=score_bc[:, U % 2],
                                               op0=ALU.add, op1=ALU.mult).then_inc(scaled_ready, 1)
                dve.wait_ge(scaled_ready, U + 1)
                nc.vector.tensor_tensor(gated[:], ps_g[U % 2][:], scaled[:], ALU.mult).then_inc(gated_ready, 1)
                dve.wait_ge(gated_ready, U + 1)
                dve.wait_ge(gu_filled, 2 * U + 2)
                if U >= 2:
                    dve.wait_ge(h_lo_ready, U - 1)
                nc.vector.tensor_tensor(h[:, U % 2], ps_u[U % 2][:], gated[:], ALU.mult).then_inc(h_ready, 1)
                if U == 5:
                    norm_x1(1, 0)
                if U == 6:
                    norm_x1(1, 1)
                woven(U, 0, att)
                woven(U, 1, att)
                if U == E + 1:
                    finish(0, 0)
                    finish(0, 1)
            finish(1, 0)
            finish(1, 1)


_INS = ['x', 'ctx_1024', 'L0_xattn_Wq', 'L0_xattn_bq', 'L0_xattn_Wk', 'L0_xattn_bk',
        'L0_ffn_router_gate', 'L0_ffn_expert_gate_up', 'L0_ffn_expert_down']
_OUTS = [((4, 256, 256), 'float32')]


def kernel(**inputs):
    import numpy as _np
    import concourse.bacc as _bacc
    from concourse import mybir as _mybir
    from concourse.bass_utils import run_bass_kernel_spmd as _run

    nc = _bacc.Bacc("TRN2", target_bir_lowering=False, num_devices=1)
    arrays, args = {}, []
    for name in _INS:
        a = _np.ascontiguousarray(inputs[name])
        arrays[f"in_{name}_dram"] = a
        args.append(nc.dram_tensor(f"in_{name}_dram", a.shape, _mybir.dt.from_np(a.dtype), kind="ExternalInput").ap())
    for i, (shape, dtype) in enumerate(_OUTS):
        dt = _mybir.dt.from_np(_np.dtype(dtype))
        args.append(nc.dram_tensor(f"out_{i}_dram", shape, dt, kind="ExternalOutput").ap())
    cross_attention_moe_kernel(nc, *args)
    r = _run(nc, [arrays], core_ids=[0])
    got = tuple(r.results[0][f"out_{i}_dram"] for i in range(len(_OUTS)))
    return got[0]
```

```python
import concourse.bass as bass
from concourse import mybir
from contextlib import ExitStack


def cross_attention_moe_kernel(
    nc: bass.Bass,
    x: bass.AP,
    ctx_feats: bass.AP,
    Wq: bass.AP,
    bq: bass.AP,
    Wk: bass.AP,
    bk: bass.AP,
    router_gate: bass.AP,
    gate_up: bass.AP,
    down: bass.AP,
    out: bass.AP,
):
    f32 = mybir.dt.float32
    f32r = mybir.dt.float32r
    ALU = mybir.AluOpType
    ACT = mybir.ActivationFunctionType
    AX = mybir.AxisListType

    P = 128
    B, L, N = x.shape
    D = Wq.shape[0]
    E = router_gate.shape[0]
    I = down.shape[1]
    EPS = 1e-5
    PAIRS = B // 2
    LT = L // P
    NT = N // P
    TP = 2 * LT
    TOK = 2 * L
    UNITS = PAIRS * E
    GU_LOADS = 4
    WARM_UP = 8
    ROUTED_FROM = 4
    ROUTER = TP * NT * 2
    EL = E // GU_LOADS

    ctx = ExitStack()
    with ctx:
        def sb(name, shape, dt=f32):
            return ctx.enter_context(nc.sbuf_tensor(name, shape, dt))

        def sem(name):
            return ctx.enter_context(nc.semaphore(name))

        x_sb = sb("x_sb", [P, B * LT, N])
        x1_sb = sb("x1_sb", [P, B * LT, N])
        out_sb = sb("out_sb", [P, B * LT, N])
        ctx_sb = sb("ctx_sb", [P, B * NT, D])
        wqk_sb = sb("wqk_sb", [P, 2, D])
        bias_sb = sb("bias_sb", [P, 2])
        gate_sb = sb("gate_sb", [E, N])
        gu_raw = sb("gu_raw", [P, E, NT, 2 * I])
        down_raw = sb("down_raw", [P, E, N])
        gu_hi = sb("gu_hi", [P, E, NT, 2, I], f32r)
        gu_lo = sb("gu_lo", [P, E, NT, 2, I], f32r)
        down_hi = sb("down_hi", [P, E, N], f32r)
        down_lo = sb("down_lo", [P, E, N], f32r)
        ident = sb("ident", [P, P])
        minus_half = sb("minus_half", [P, TP])
        expert_no = sb("expert_no", [P, TP, E], mybir.dt.int32)
        expert_id = sb("expert_id", [P, TP, E])
        wqkT = sb("wqkT", [P, 2, P])
        gateT = sb("gateT", [P, NT, 2, E], f32r)
        ctxT = sb("ctxT", [P, 2 * N])
        qT = sb("qT", [P, 2 * N])
        kT = sb("kT", [P, 2 * N])
        stats = sb("stats", [P, TP, 6])
        mean_var = sb("mean_var", [P, TP, 2])
        var_eps = sb("var_eps", [P, TP])
        rstd = sb("rstd", [P, TP])
        ln = sb("ln", [P, TP, N])
        lnT = sb("lnT", [P, 2, NT, L])
        neg_max = sb("neg_max", [P, TP])
        probs = sb("probs", [P, TP, N])
        denom = sb("denom", [P, TP])
        rdenom = sb("rdenom", [P, TP])
        probsT = sb("probsT", [P, 2, NT, N])
        stats2 = sb("stats2", [P, TP, 6])
        mean_var2 = sb("mean_var2", [P, TP, 2])
        var_eps2 = sb("var_eps2", [P, TP])
        rstd2 = sb("rstd2", [P, TP])
        hs = sb("hs", [P, TP, N])
        hsT_hi = sb("hsT_hi", [P, PAIRS, NT, TOK], f32r)
        hsT_lo = sb("hsT_lo", [P, PAIRS, NT, TOK], f32r)
        logits_lo = sb("logits_lo", [P, TP, E])
        logits = sb("logits", [P, TP, E])
        top = sb("top", [P, TP, 8])
        top_no = sb("top_no", [P, TP, 8], mybir.dt.uint32)
        top_id = sb("top_id", [P, TP, 2])
        gap = sb("gap", [P, TP])
        e_gap = sb("e_gap", [P, TP])
        one_e = sb("one_e", [P, TP])
        inv_e = sb("inv_e", [P, TP])
        w_top = sb("w_top", [P, TP, 2])
        is_top = sb("is_top", [P, 2, TP, E])
        w_is_top = sb("w_is_top", [P, 2, TP, E])
        scores = sb("scores", [P, TP, E])
        scoresT = sb("scoresT", [E, TOK])
        score_row = sb("score_row", [1, PAIRS, E, TOK])
        score_bc = sb("score_bc", [P, 2, TOK])
        tanh_g = sb("tanh_g", [P, 2, TOK])
        scaled = sb("scaled", [P, TOK])
        gated = sb("gated", [P, TOK])
        h = sb("h", [P, 2, TOK])
        h_hi = sb("h_hi", [P, 2, TOK], f32r)
        h_lo = sb("h_lo", [P, 2, TOK], f32r)

        def bank(name, shape):
            return ctx.enter_context(nc.psum_tensor(name, shape, f32))

        ps_g = [bank(f"ps_g{i}", [P, TOK]) for i in range(2)]
        ps_u = [bank(f"ps_u{i}", [P, TOK]) for i in range(2)]
        ps_out = [bank(f"ps_out{i}", [P, 2 * N]) for i in range(2)]
        ps_a = [bank(f"ps_a{i}", [P, TOK]) for i in range(2)]

        x_in = [sem(f"x_in{p}") for p in range(PAIRS)]
        ctx_in = [sem(f"ctx_in{p}") for p in range(PAIRS)]
        wqk_in = sem("wqk_in")
        small_in = sem("small_in")
        gu_in = [sem(f"gu_in{i}") for i in range(GU_LOADS)]
        down_in = [sem(f"down_in{i}") for i in range(2)]
        consts = sem("consts")
        att_filled = sem("att_filled")
        act_drained = sem("act_drained")
        dve_drained = sem("dve_drained")
        dve_step = sem("dve_step")
        var_ready = sem("var_ready")
        rstd_ready = sem("rstd_ready")
        ln_ready = sem("ln_ready")
        max_ready = sem("max_ready")
        exp_ready = sem("exp_ready")
        probs_ready = sem("probs_ready")
        hi_ready = sem("hi_ready")
        gap_ready = sem("gap_ready")
        egap_ready = sem("egap_ready")
        scores_ready = sem("scores_ready")
        row_ready = sem("row_ready")
        gu_hi_ready = sem("gu_hi_ready")
        gu_lo_ready = sem("gu_lo_ready")
        down_hi_ready = sem("down_hi_ready")
        down_lo_ready = sem("down_lo_ready")
        gu_filled = sem("gu_filled")
        tanh_ready = sem("tanh_ready")
        bc_ready = sem("bc_ready")
        scaled_ready = sem("scaled_ready")
        gated_ready = sem("gated_ready")
        h_ready = sem("h_ready")
        h_hi_ready = sem("h_hi_ready")
        h_lo_ready = sem("h_lo_ready")
        down_done = sem("down_done")
        out_ps0_ready = sem("out_ps0_ready")
        out_ready = sem("out_ready")
        stored = [sem(f"stored{b}") for b in range(B)]

        BANKS = [ps_out[0], ps_g[0], ps_u[0], ps_g[1], ps_u[1], ps_out[1], ps_a[0], ps_a[1]]
        READER = {"wqkT": "dve", "gateT": "dve", "ctxT": "act", "q": "act", "k": "act", "E0": "act", "E1": "act",
                  "LT0": "dve", "LT1": "dve", "AT0": "act", "AT1": "act", "M0": "dve", "M1": "dve",
                  "H0": "dve", "H1": "dve", "logits": "dve", "scoresT": "act"}
        FILLS = [(0, "ctxT"), (0, "wqkT"), (0, "q"), (0, "k"), (0, "gateT"), (0, "E0"), (0, "E1"), (0, "LT0"),
                 (0, "LT1"), (0, "AT0"), (0, "AT1"), (0, "M0"), (0, "M1"), (1, "ctxT"), (1, "q"), (1, "k"),
                 (0, "H0"), (0, "H1"), (1, "E0"), (1, "E1"), (0, "logits"), (0, "scoresT"), (1, "LT0"), (1, "LT1"),
                 (1, "AT0"), (1, "AT1"), (1, "M0"), (1, "M1"), (1, "H0"), (1, "H1"), (1, "logits"), (1, "scoresT")]
        BANK = {}
        for use in FILLS:
            in_six = use[0] == 0 and use[1] not in ("wqkT", "gateT", "logits", "scoresT")
            turn = sum((b < 6) == in_six for b in BANK.values())
            BANK[use] = turn % 6 if in_six else 6 + turn % 2

        def bank_of(p, name):
            return BANKS[BANK[p, name]]

        def filled(p, name):
            return FILLS.index((p, name)) + 1

        def drain_count(p, name):
            return sum(READER[n] == READER[name] for _, n in FILLS[:filled(p, name)])

        def wait_drained(eng, p, name):
            eng.wait_ge(act_drained if READER[name] == "act" else dve_drained, drain_count(p, name))

        def wait_bank_free(eng, p, name):
            before = [u for u in FILLS[:filled(p, name) - 1] if BANK[u] == BANK[p, name]]
            if before:
                wait_drained(eng, *before[-1])

        WOVEN = {1: (["LT0", "LT1", "AT0", "AT1"], ["M0", "M1"]), 4: (["H0"], ["H1"]), 7: (["scoresT"], [])}
        ROUTED = {0: 0, 6: 1}

        def gu_src(e):
            return gu_raw[:, e].rearrange("p k (i two) -> p k two i", two=2)

        block = ctx.enter_context(nc.Block())

        @block.sync
        def _(sp):
            def load_gu(i):
                es = slice(i * EL, (i + 1) * EL)
                sp.dma_start(gu_raw[:, es], gate_up[es].rearrange("e (k q) f -> q e k f", q=P)).then_inc(gu_in[i], 16)

            def load_rows(dst, src, p, done):
                sp.dma_start(dst[:, p * TP:(p + 1) * TP, :],
                             src[2 * p:2 * p + 2].rearrange("b (t q) n -> q (b t) n", q=P)).then_inc(done, 16)

            load_rows(ctx_sb, ctx_feats, 0, ctx_in[0])
            load_rows(x_sb, x, 0, x_in[0])
            load_gu(0)
            load_gu(1)
            load_rows(ctx_sb, ctx_feats, 1, ctx_in[1])
            load_rows(x_sb, x, 1, x_in[1])
            load_gu(2)
            load_gu(3)
            for p in range(PAIRS):
                wait_drained(sp, p, "scoresT")
                sp.dma_start(score_row[0:1, p], scoresT[:]).then_inc(row_ready, 16)
            for b in range(B):
                sp.wait_ge(out_ready, b + 1)
                sp.dma_start(out[b].rearrange("(t q) n -> q t n", q=P),
                             out_sb[:, b * LT:(b + 1) * LT, :]).then_inc(stored[b], 16)
            for b in range(B):
                sp.wait_ge(stored[b], 16)

        @block.gpsimd
        def _(pool):
            nc.gpsimd.memset(ident[:], 0.0).then_inc(consts, 1)
            nc.gpsimd.memset(minus_half[:], -0.5).then_inc(consts, 1)
            pool.wait_ge(consts, 1)
            nc.gpsimd.affine_select(out=ident[:], in_=ident[:], compare_op=ALU.not_equal, fill=1.0, base=0,
                                    pattern=[[-1, P]], channel_multiplier=1).then_inc(consts, 1)
            nc.gpsimd.iota(expert_no[:], pattern=[[0, TP], [1, E]], base=0, channel_multiplier=0).then_inc(consts, 1)

            def inv_sqrt(n, src, dst):
                pool.wait_ge(var_ready, n)
                nc.gpsimd.tensor_tensor(dst[:], src[:], minus_half[:], ALU.pow).then_inc(rstd_ready, 1)

            def inv_sqrt_batch(n, bi):
                pool.wait_ge(var_ready, n)
                t = slice(bi * LT, (bi + 1) * LT)
                nc.gpsimd.tensor_tensor(rstd2[:, t], var_eps2[:, t], minus_half[:, t], ALU.pow).then_inc(rstd_ready, 1)

            def gu_lo_part(e):
                pool.wait_ge(gu_hi_ready, e + 1)
                nc.gpsimd.tensor_tensor(gu_lo[:, e], gu_src(e), gu_hi[:, e].bitcast(f32),
                                        ALU.subtract).then_inc(gu_lo_ready, 1)

            def down_lo_part(e):
                pool.wait_ge(down_hi_ready, e + 1)
                nc.gpsimd.tensor_tensor(down_lo[:, e], down_raw[:, e], down_hi[:, e].bitcast(f32),
                                        ALU.subtract).then_inc(down_lo_ready, 1)

            def broadcast(U):
                p, e = divmod(U, E)
                if e == 0:
                    pool.wait_ge(row_ready, 16 * (p + 1))
                if U >= 2:
                    pool.wait_ge(scaled_ready, U - 1)
                nc.gpsimd.partition_broadcast(score_bc[:, U % 2], score_row[0:1, p, e], P).then_inc(bc_ready, 1)

            inv_sqrt(1, var_eps, rstd)
            gu_lo_part(0)
            inv_sqrt_batch(2, 0)
            inv_sqrt_batch(3, 1)
            gu_lo_part(1)
            gu_lo_part(2)
            down_lo_part(0)
            inv_sqrt(4, var_eps, rstd)
            gu_lo_part(3)
            broadcast(0)
            for U in range(UNITS):
                if U + 1 < UNITS:
                    broadcast(U + 1)
                if U == 1:
                    inv_sqrt_batch(5, 0)
                if U == 2:
                    inv_sqrt_batch(6, 1)
                pool.wait_ge(h_hi_ready, U + 1)
                if U >= 2:
                    pool.wait_ge(down_done, U - 1)
                nc.gpsimd.tensor_tensor(h_lo[:, U % 2], h[:, U % 2], h_hi[:, U % 2].bitcast(f32),
                                        ALU.subtract).then_inc(h_lo_ready, 1)
                if U + 1 < E:
                    down_lo_part(U + 1)
                if U + 4 < E:
                    gu_lo_part(U + 4)

        @block.tensor
        def _(pe):
            def att(p, name):
                wait_bank_free(pe, p, name)
                dst = bank_of(p, name)
                if name == "ctxT":
                    pe.wait_ge(ctx_in[p], 16)
                    for j in range(TP):
                        last = nc.tensor.transpose(dst[:, j * P:(j + 1) * P], ctx_sb[:, p * TP + j], ident[:])
                elif name in ("q", "k"):
                    wait_drained(pe, p, "ctxT")
                    last = nc.tensor.matmul(dst[:], wqkT[:, "qk".index(name)], ctxT[:], start=True, stop=True)
                elif name[0] == "E":
                    wait_drained(pe, p, "q")
                    wait_drained(pe, p, "k")
                    o = int(name[1]) * N
                    for t in range(NT):
                        last = nc.tensor.matmul(dst[:, t * N:(t + 1) * N], qT[:, o + t * P:o + (t + 1) * P],
                                                kT[:, o:o + N], start=True, stop=True)
                elif name[:2] in ("LT", "AT"):
                    bi = int(name[2])
                    if name[0] == "L":
                        src = ln
                        pe.wait_ge(ln_ready, p * 2 * TP + (bi + 1) * LT)
                    else:
                        src = probs
                        pe.wait_ge(probs_ready, 2 * p + bi + 1)
                    v = dst[:].rearrange("q (k r) -> q k r", k=NT)
                    for t in range(2):
                        for c in range(NT):
                            last = nc.tensor.transpose(v[:, c, t * P:(t + 1) * P],
                                                       src[:, bi * LT + t, c * P:(c + 1) * P], ident[:])
                elif name[0] == "M":
                    bi = int(name[1])
                    wait_drained(pe, p, f"LT{bi}")
                    wait_drained(pe, p, f"AT{bi}")
                    for t in range(LT):
                        for c in range(NT):
                            last = nc.tensor.matmul(dst[:, t * N:(t + 1) * N], lnT[:, bi, c, t * P:(t + 1) * P],
                                                    probsT[:, bi, c], start=(c == 0), stop=(c == NT - 1))
                elif name[0] == "H":
                    bi = int(name[1])
                    pe.wait_ge(ln_ready, p * 2 * TP + TP + (bi + 1) * LT)
                    v = dst[:].rearrange("q (k r) -> q k r", k=NT)
                    for t in range(LT):
                        for c in range(NT):
                            last = nc.tensor.transpose(v[:, c, t * P:(t + 1) * P],
                                                       hs[:, bi * LT + t, c * P:(c + 1) * P], ident[:])
                else:
                    pe.wait_ge(scores_ready, p + 1)
                    for j in range(TP):
                        last = nc.tensor.transpose(dst[0:E, j * P:(j + 1) * P], scores[:, j], ident[:])
                last.then_inc(att_filled, 1)

            def router_product(p, n):
                j, (part, c) = n // (2 * NT), divmod(n % (2 * NT), NT)
                if n == 0:
                    wait_bank_free(pe, p, "logits")
                if n == 0 or (p, n) == (0, NT):
                    wait_drained(pe, p, "H1")
                ins = nc.tensor.matmul(bank_of(p, "logits")[:, j * 2 * E:(j + 1) * 2 * E],
                                       (hsT_hi, hsT_lo)[part][:, p, c, j * P:(j + 1) * P],
                                       gateT[:, c].rearrange("q s e -> q (s e)"),
                                       start=(n % (2 * NT) == 0), stop=(n % (2 * NT) == 2 * NT - 1))
                if n == ROUTER - 1:
                    ins.then_inc(att_filled, 1)

            pe.wait_ge(consts, 4)
            for _ in range(WARM_UP):
                nc.tensor.matmul(ps_out[0][:, 0:P], ident[:], ident[:], start=True, stop=True)
            att(0, "ctxT")
            pe.wait_ge(wqk_in, 32)
            for i in range(2):
                last = nc.tensor.transpose(bank_of(0, "wqkT")[:, i * P:(i + 1) * P], wqk_sb[:, i], ident[:])
            last.then_inc(att_filled, 1)
            wait_drained(pe, 0, "wqkT")
            for name in ("q", "k"):
                att(0, name)
            pe.wait_ge(small_in, 16 * 3)
            for c in range(NT):
                last = nc.tensor.transpose(bank_of(0, "gateT")[:, c * E:(c + 1) * E], gate_sb[:, c * P:(c + 1) * P],
                                           ident[0:E, 0:E])
            last.then_inc(att_filled, 1)
            for name in ("E0", "E1", "LT0", "LT1", "AT0", "AT1", "M0", "M1"):
                att(0, name)
            for name in ("ctxT", "q", "k"):
                att(1, name)
            att(0, "H0")
            att(0, "H1")
            att(1, "E0")
            att(1, "E1")

            def gate_up_unit(U):
                p, e = divmod(U, E)
                if e == 0:
                    pe.wait_ge(hi_ready, 2 * (p + 1))
                if p == 0:
                    pe.wait_ge(gu_lo_ready, e + 1)
                if U >= 2:
                    pe.wait_ge(h_ready, U - 1)
                terms = [(w, a, c) for w, a in ((gu_lo, hsT_hi), (gu_hi, hsT_hi), (gu_hi, hsT_lo)) for c in range(NT)]
                steps = 2 * len(terms)
                for half, dst in enumerate((ps_g[U % 2], ps_u[U % 2])):
                    for i, (w, a, c) in enumerate(terms):
                        if e == 0 and half == 0 and i == 2 * NT:
                            wait_drained(pe, p, "H1")
                        last = nc.tensor.matmul(dst[:], w[:, e, c, half], a[:, p, c],
                                                start=(i == 0), stop=(i == len(terms) - 1))
                        if i == len(terms) - 1:
                            last.then_inc(gu_filled, 1)
                        if U in ROUTED and ROUTED_FROM <= half * len(terms) + i:
                            n = half * len(terms) + i - ROUTED_FROM
                            for r in range(2 * n, min(2 * n + 2, ROUTER)):
                                router_product(ROUTED[U], r)

            def down_unit(U):
                p, e = divmod(U, E)
                pe.wait_ge(h_lo_ready, U + 1)
                if p == 0:
                    pe.wait_ge(down_lo_ready, e + 1)
                if e == 0 and p > 0:
                    pe.wait_ge(out_ready, 2 * p)
                for j in range(TP):
                    cols = slice(j * P, (j + 1) * P)
                    dst = ps_out[j // 2][:, (j % 2) * N:(j % 2 + 1) * N]
                    terms = ((h_lo, down_hi), (h_hi, down_lo), (h_hi, down_hi))
                    for i, (a, w) in enumerate(terms):
                        last = nc.tensor.matmul(dst, a[:, U % 2, cols], w[:, e],
                                                start=(e == 0 and i == 0 and j % 2 == 0),
                                                stop=(e == E - 1 and i == 2), skip_group_check=True)
                    if j == TP - 1:
                        last.then_inc(down_done, 1)
                    elif e == E - 1 and j % 2 == 1:
                        last.then_inc(out_ps0_ready, 1)

            for U in range(UNITS + 2):
                before_down, after_down = WOVEN.get(U, ([], []))
                if U < UNITS:
                    gate_up_unit(U)
                if U == 1:
                    att(0, "scoresT")
                for name in before_down:
                    att(1, name)
                if U >= 2:
                    down_unit(U - 2)
                for name in after_down:
                    att(1, name)

        @block.scalar
        def _(act):
            act.dma_start(wqk_sb[:, 0], Wq).then_inc(wqk_in, 16)
            act.dma_start(wqk_sb[:, 1], Wk).then_inc(wqk_in, 16)
            act.dma_start(bias_sb[:, 0:1], bq.rearrange("(d o) -> d o", o=1)).then_inc(small_in, 16)
            act.dma_start(bias_sb[:, 1:2], bk.rearrange("(d o) -> d o", o=1)).then_inc(small_in, 16)
            act.dma_start(gate_sb[:], router_gate).then_inc(small_in, 16)
            nc.scalar.preload_act_table(ACT.Exp)
            for i in range(2):
                es = slice(i * E // 2, (i + 1) * E // 2)
                act.dma_start(down_raw[:, es], down[es].rearrange("e i n -> i e n")).then_inc(down_in[i], 16)

            def att(p, name):
                if name in ("ctxT", "AT0", "AT1"):
                    src = bank_of(p, name)
                    act.wait_ge(att_filled, filled(p, name))
                    if name == "ctxT":
                        nc.scalar.copy(ctxT[:], src[:]).then_inc(act_drained, 1)
                    else:
                        nc.scalar.copy(probsT[:, int(name[2])].rearrange("q k r -> q (k r)"), src[:]).then_inc(act_drained, 1)
                elif name in ("q", "k"):
                    act.wait_ge(att_filled, filled(p, name))
                    act.wait_ge(small_in, 16 * 3)
                    i = "qk".index(name)
                    nc.scalar.activation((qT, kT)[i][:], bank_of(p, name)[:], ACT.Identity,
                                         bias=bias_sb[:, i:i + 1]).then_inc(act_drained, 1)
                elif name in ("E0", "E1"):
                    bi = int(name[1])
                    act.wait_ge(max_ready, 2 * p + bi + 1)
                    src = bank_of(p, name)
                    for t in range(2):
                        j = 2 * bi + t
                        nc.scalar.activation(probs[:, j], src[:, t * N:(t + 1) * N], ACT.Exp,
                                             bias=neg_max[:, j:j + 1],
                                             accum_out=denom[:, j:j + 1]).then_inc(exp_ready, 1)
                    act.wait_ge(exp_ready, 4 * p + 2 * bi + 2)
                    act.sem_inc(act_drained, 1)
                elif name in ("H0", "H1"):
                    bi = int(name[1])
                    act.wait_ge(att_filled, filled(p, name))
                    v = bank_of(p, name)[:].rearrange("q (k r) -> q k r", k=NT)
                    nc.scalar.copy(hsT_hi[:, p, :, bi * L:(bi + 1) * L], v).then_inc(hi_ready, 1)
                elif name == "logits":
                    act.wait_ge(gap_ready, p + 1)
                    nc.scalar.activation(e_gap[:], gap[:], ACT.Exp).then_inc(egap_ready, 1)
                elif name == "scoresT":
                    act.wait_ge(att_filled, filled(p, name))
                    if p > 0:
                        act.wait_ge(row_ready, 16 * p)
                    nc.scalar.copy(scoresT[:], bank_of(p, name)[0:E, :]).then_inc(act_drained, 1)

            for name in ("ctxT", "q", "k", "E0", "E1", "AT0", "AT1"):
                att(0, name)
            for name in ("ctxT", "q", "k"):
                att(1, name)
            att(0, "H0")
            att(0, "H1")
            att(1, "E0")
            att(1, "E1")
            for U in range(UNITS):
                act.wait_ge(gu_filled, 2 * U + 1)
                if U >= 2:
                    act.wait_ge(scaled_ready, U - 1)
                nc.scalar.activation(tanh_g[:, U % 2], ps_g[U % 2][:], ACT.Tanh, scale=0.5).then_inc(tanh_ready, 1)
                if U == 0:
                    att(0, "logits")
                    att(0, "scoresT")
                    att(1, "AT0")
                    att(1, "AT1")
                if U == 4:
                    att(1, "H0")
                if U == 5:
                    att(1, "H1")
                if U == 7:
                    att(1, "logits")
                    att(1, "scoresT")
                act.wait_ge(h_ready, U + 1)
                if U >= 2:
                    act.wait_ge(down_done, U - 1)
                nc.scalar.copy(h_hi[:, U % 2], h[:, U % 2]).then_inc(h_hi_ready, 1)

        @block.vector
        def _(dve):
            steps = [0]

            def step(ins):
                ins.then_inc(dve_step, 1)
                steps[0] += 1
                dve.wait_ge(dve_step, steps[0])

            def mean_and_var(src, tiles, st, mv, ve):
                for i, j in enumerate(tiles):
                    ins = nc.vector.bn_stats(st[:, j], src(j))
                    ins.then_inc(dve_step, 1)
                    steps[0] += 1
                dve.wait_ge(dve_step, steps[0])
                for j in tiles:
                    ins = nc.vector.bn_aggr(mv[:, j], st[:, j])
                    ins.then_inc(dve_step, 1)
                    steps[0] += 1
                dve.wait_ge(dve_step, steps[0])
                t = slice(tiles[0], tiles[-1] + 1)
                nc.vector.tensor_scalar_add(ve[:, t], mv[:, t, 1], EPS).then_inc(var_ready, 1)

            def normalise(n, src, tiles, mv, rs, dst):
                dve.wait_ge(rstd_ready, n)
                for j in tiles:
                    nc.vector.tensor_scalar(dst[:, j], src(j), mv[:, j, 0:1], rs[:, j:j + 1],
                                            ALU.subtract, ALU.mult).then_inc(ln_ready, 1)

            def att(p, name):
                def xt(j):
                    return x_sb[:, p * TP + j]

                def x1t(j):
                    return x1_sb[:, p * TP + j]

                if name == "ctxT":
                    dve.wait_ge(x_in[p], 16)
                    mean_and_var(xt, list(range(TP)), stats, mean_var, var_eps)
                elif name in ("E0", "E1"):
                    bi = int(name[1])
                    dve.wait_ge(att_filled, filled(p, name))
                    nc.vector.tensor_reduce(neg_max[:, 2 * bi:2 * bi + 2],
                                            bank_of(p, name)[:].rearrange("q (t n) -> q t n", t=2),
                                            AX.X, ALU.max, negate=True).then_inc(max_ready, 1)
                elif name in ("LT0", "LT1"):
                    bi = int(name[2])
                    dve.wait_ge(att_filled, filled(p, name))
                    nc.vector.tensor_copy(lnT[:, bi].rearrange("q k r -> q (k r)"),
                                          bank_of(p, name)[:]).then_inc(dve_drained, 1)
                elif name in ("AT0", "AT1"):
                    bi = int(name[2])
                    dve.wait_ge(exp_ready, 4 * p + 2 * bi + 2)
                    step(nc.vector.reciprocal(rdenom[:, 2 * bi:2 * bi + 2], denom[:, 2 * bi:2 * bi + 2]))
                    for t in range(2):
                        j = 2 * bi + t
                        last = nc.vector.tensor_scalar(probs[:, j], probs[:, j], rdenom[:, j:j + 1], None, ALU.mult)
                    last.then_inc(probs_ready, 1)
                elif name in ("M0", "M1"):
                    bi = int(name[1])
                    t0 = p * TP + bi * LT
                    dve.wait_ge(att_filled, filled(p, name))
                    ins = nc.vector.tensor_tensor(x1_sb[:, t0:t0 + LT].rearrange("q t n -> q (t n)"),
                                                  bank_of(p, name)[:],
                                                  x_sb[:, t0:t0 + LT].rearrange("q t n -> q (t n)"), ALU.add)
                    ins.then_inc(dve_drained, 1)
                    dve.wait_ge(dve_drained, drain_count(p, name))
                    mean_and_var(x1t, [bi * LT, bi * LT + 1], stats2, mean_var2, var_eps2)
                elif name in ("H0", "H1"):
                    bi = int(name[1])
                    dve.wait_ge(hi_ready, 2 * p + bi + 1)
                    v = bank_of(p, name)[:].rearrange("q (k r) -> q k r", k=NT)
                    cols = slice(bi * L, (bi + 1) * L)
                    nc.vector.tensor_tensor(hsT_lo[:, p, :, cols], v, hsT_hi[:, p, :, cols].bitcast(f32),
                                            ALU.subtract).then_inc(dve_drained, 1)
                elif name == "logits":
                    route(p)

            def norm_x1(p, bi):
                normalise(3 * p + 2 + bi, lambda j: x1_sb[:, p * TP + j], [bi * LT, bi * LT + 1],
                          mean_var2, rstd2, hs)

            def route(p):
                dve.wait_ge(att_filled, filled(p, "logits"))
                parts = bank_of(p, "logits")[:, 0:TP * 2 * E].rearrange("q (t s e) -> q t s e", t=TP, s=2)
                step(nc.vector.tensor_copy(logits_lo[:], parts[:, :, 1]))
                nc.vector.tensor_tensor(logits[:], parts[:, :, 0], logits_lo[:], ALU.add).then_inc(dve_drained, 1)
                dve.wait_ge(dve_drained, drain_count(p, "logits"))
                for j in range(TP):
                    ins = nc.vector.max(top[:, j], logits[:, j])
                    ins.then_inc(dve_step, 1)
                    steps[0] += 1
                dve.wait_ge(dve_step, steps[0])
                nc.vector.tensor_tensor(gap[:], top[:, :, 1], top[:, :, 0], ALU.subtract).then_inc(gap_ready, 1)
                for j in range(TP):
                    ins = nc.vector.max_index(top_no[:, j], top[:, j], logits[:, j])
                    ins.then_inc(dve_step, 1)
                    steps[0] += 1
                dve.wait_ge(dve_step, steps[0])
                step(nc.vector.tensor_copy(top_id[:], top_no[:, :, 0:2]))
                for r in range(2):
                    ins = nc.vector.tensor_tensor(is_top[:, r], expert_id[:],
                                                  top_id[:, :, r:r + 1].broadcast_to([P, TP, E]), ALU.is_equal)
                    ins.then_inc(dve_step, 1)
                    steps[0] += 1
                dve.wait_ge(egap_ready, p + 1)
                step(nc.vector.tensor_scalar(one_e[:], e_gap[:], 1.0, 2.0, ALU.add, ALU.mult))
                step(nc.vector.reciprocal(w_top[:, :, 0], one_e[:]))
                step(nc.vector.tensor_tensor(w_top[:, :, 1], w_top[:, :, 0], e_gap[:], ALU.mult))
                for r in range(2):
                    ins = nc.vector.tensor_tensor(w_is_top[:, r], is_top[:, r],
                                                  w_top[:, :, r:r + 1].broadcast_to([P, TP, E]), ALU.mult)
                    ins.then_inc(dve_step, 1)
                    steps[0] += 1
                dve.wait_ge(dve_step, steps[0])
                nc.vector.tensor_tensor(scores[:], w_is_top[:, 0], w_is_top[:, 1], ALU.add).then_inc(scores_ready, 1)

            def split_gu(e):
                if e % EL == 0:
                    dve.wait_ge(gu_in[e // EL], 16)
                nc.vector.tensor_copy(gu_hi[:, e], gu_src(e)).then_inc(gu_hi_ready, 1)

            def split_down(e):
                if e % (E // 2) == 0:
                    dve.wait_ge(down_in[e // (E // 2)], 16)
                nc.vector.tensor_copy(down_hi[:, e], down_raw[:, e]).then_inc(down_hi_ready, 1)

            dve.wait_ge(consts, 4)
            step(nc.vector.tensor_copy(expert_id[:], expert_no[:]))
            dve.wait_ge(att_filled, 2)
            nc.vector.tensor_copy(wqkT[:].rearrange("q a b -> q (a b)"),
                                  bank_of(0, "wqkT")[:, 0:2 * P]).then_inc(dve_drained, 1)
            att(0, "ctxT")
            normalise(1, lambda j: x_sb[:, j], list(range(TP)), mean_var, rstd, ln)
            dve.wait_ge(att_filled, filled(0, "gateT"))
            gate_ps = bank_of(0, "gateT")[:, 0:NT * E].rearrange("q (c e) -> q c e", c=NT)
            step(nc.vector.tensor_copy(gateT[:, :, 0], gate_ps))
            nc.vector.tensor_tensor(gateT[:, :, 1], gate_ps, gateT[:, :, 0].bitcast(f32),
                                    ALU.subtract).then_inc(dve_drained, 1)
            for name in ("E0", "E1", "AT0", "LT0", "AT1", "LT1"):
                att(0, name)
            for e in range(3):
                split_gu(e)
            att(0, "M0")
            att(0, "M1")
            norm_x1(0, 0)
            norm_x1(0, 1)
            att(0, "H0")
            att(0, "H1")
            att(1, "E0")
            att(1, "E1")
            att(1, "ctxT")
            split_down(0)
            split_gu(3)
            att(0, "logits")
            normalise(4, lambda j: x_sb[:, TP + j], list(range(TP)), mean_var, rstd, ln)
            for name in ("AT0", "AT1", "LT0", "LT1"):
                att(1, name)
            for e in range(1, E):
                split_down(e)

            def finish(p, i):
                t0 = p * TP + i * LT
                if i == 0:
                    dve.wait_ge(out_ps0_ready, p + 1)
                else:
                    dve.wait_ge(down_done, (p + 1) * E)
                nc.vector.tensor_tensor(out_sb[:, t0:t0 + LT], ps_out[i][:].rearrange("q (t n) -> q t n", t=LT), x1_sb[:, t0:t0 + LT],
                                        ALU.add).then_inc(out_ready, 1)

            for U in range(UNITS):
                dve.wait_ge(tanh_ready, U + 1)
                dve.wait_ge(bc_ready, U + 1)
                nc.vector.scalar_tensor_tensor(out=scaled[:], in0=tanh_g[:, U % 2], scalar=1.0, in1=score_bc[:, U % 2],
                                               op0=ALU.add, op1=ALU.mult).then_inc(scaled_ready, 1)
                dve.wait_ge(scaled_ready, U + 1)
                nc.vector.tensor_tensor(gated[:], ps_g[U % 2][:], scaled[:], ALU.mult).then_inc(gated_ready, 1)
                dve.wait_ge(gated_ready, U + 1)
                dve.wait_ge(gu_filled, 2 * U + 2)
                if U >= 2:
                    dve.wait_ge(h_lo_ready, U - 1)
                nc.vector.tensor_tensor(h[:, U % 2], ps_u[U % 2][:], gated[:], ALU.mult).then_inc(h_ready, 1)
                if U == 0:
                    att(1, "M0")
                    for e in range(4, E):
                        split_gu(e)
                if U == 1:
                    att(1, "M1")
                if U == 2:
                    norm_x1(1, 0)
                    norm_x1(1, 1)
                if U == 4:
                    att(1, "H0")
                    att(1, "H1")
                if U == 6:
                    att(1, "logits")
                if U == E + 1:
                    finish(0, 0)
                    finish(0, 1)
            finish(1, 0)
            finish(1, 1)


_INS = ['x', 'ctx_1024', 'L0_xattn_Wq', 'L0_xattn_bq', 'L0_xattn_Wk', 'L0_xattn_bk',
        'L0_ffn_router_gate', 'L0_ffn_expert_gate_up', 'L0_ffn_expert_down']
_OUTS = [((4, 256, 256), 'float32')]


def kernel(**inputs):
    import numpy as _np
    import concourse.bacc as _bacc
    from concourse import mybir as _mybir
    from concourse.bass_utils import run_bass_kernel_spmd as _run

    nc = _bacc.Bacc("TRN2", target_bir_lowering=False, num_devices=1)
    arrays, args = {}, []
    for name in _INS:
        a = _np.ascontiguousarray(inputs[name])
        arrays[f"in_{name}_dram"] = a
        args.append(nc.dram_tensor(f"in_{name}_dram", a.shape, _mybir.dt.from_np(a.dtype), kind="ExternalInput").ap())
    for i, (shape, dtype) in enumerate(_OUTS):
        dt = _mybir.dt.from_np(_np.dtype(dtype))
        args.append(nc.dram_tensor(f"out_{i}_dram", shape, dt, kind="ExternalOutput").ap())
    cross_attention_moe_kernel(nc, *args)
    r = _run(nc, [arrays], core_ids=[0])
    got = tuple(r.results[0][f"out_{i}_dram"] for i in range(len(_OUTS)))
    return got[0]
```

```python
import concourse.bass as bass
from concourse import mybir
from contextlib import ExitStack


def cross_attention_moe_kernel(
    nc: bass.Bass,
    x: bass.AP,
    ctx_feats: bass.AP,
    Wq: bass.AP,
    bq: bass.AP,
    Wk: bass.AP,
    bk: bass.AP,
    router_gate: bass.AP,
    gate_up: bass.AP,
    down: bass.AP,
    out: bass.AP,
):
    f32 = mybir.dt.float32
    f32r = mybir.dt.float32r
    ALU = mybir.AluOpType
    ACT = mybir.ActivationFunctionType
    AX = mybir.AxisListType

    P = 128
    B, L, N = x.shape
    D = Wq.shape[0]
    E = router_gate.shape[0]
    I = down.shape[1]
    EPS = 1e-5
    PAIRS = B // 2
    LT = L // P
    NT = N // P
    TP = 2 * LT
    TOK = 2 * L
    UNITS = PAIRS * E
    GU_LOADS = 4
    WARM_UP = 8
    EL = E // GU_LOADS

    ctx = ExitStack()
    with ctx:
        def sb(name, shape, dt=f32):
            return ctx.enter_context(nc.sbuf_tensor(name, shape, dt))

        def sem(name):
            return ctx.enter_context(nc.semaphore(name))

        x_sb = sb("x_sb", [P, B * LT, N])
        x1_sb = sb("x1_sb", [P, B * LT, N])
        ctx_sb = sb("ctx_sb", [P, B * NT, D])
        wqk_sb = sb("wqk_sb", [P, 2, D])
        bias_sb = sb("bias_sb", [P, 2])
        gate_sb = sb("gate_sb", [E, N])
        gu_raw = sb("gu_raw", [P, E, NT, 2 * I])
        down_raw = sb("down_raw", [P, E, N])
        gu_hi = sb("gu_hi", [P, E, NT, 2, I], f32r)
        gu_lo = sb("gu_lo", [P, E, NT, 2, I], f32r)
        down_hi = sb("down_hi", [P, E, N], f32r)
        down_lo = sb("down_lo", [P, E, N], f32r)
        warm = sb("warm", [P, P])
        ident = sb("ident", [P, P])
        minus_half = sb("minus_half", [P, TP])
        expert_no = sb("expert_no", [P, TP, E], mybir.dt.int32)
        expert_id = sb("expert_id", [P, TP, E])
        wqkT = sb("wqkT", [P, 2, P])
        gateT = sb("gateT", [P, NT, 2, E], f32r)
        ctxT = sb("ctxT", [P, 2 * N])
        qT = sb("qT", [P, 2 * N])
        kT = sb("kT", [P, 2 * N])
        stats = sb("stats", [P, TP, 6])
        mean_var = sb("mean_var", [P, TP, 2])
        var_eps = sb("var_eps", [P, TP])
        rstd = sb("rstd", [P, TP])
        neg_mr = sb("neg_mr", [P, TP])
        ln = sb("ln", [P, TP, N])
        lnT = sb("lnT", [P, 2, NT, L])
        neg_max = sb("neg_max", [P, TP])
        probs = sb("probs", [P, TP, N])
        denom = sb("denom", [P, TP])
        rdenom = sb("rdenom", [P, TP])
        probsT = sb("probsT", [P, 2, NT, N])
        stats2 = sb("stats2", [P, TP, 6])
        mean_var2 = sb("mean_var2", [P, TP, 2])
        var_eps2 = sb("var_eps2", [P, TP])
        rstd2 = sb("rstd2", [P, TP])
        hs = sb("hs", [P, TP, N])
        hsT_hi = sb("hsT_hi", [P, PAIRS, NT, TOK], f32r)
        hsT_lo = sb("hsT_lo", [P, PAIRS, NT, TOK], f32r)
        logitsT = sb("logitsT", [2 * E, TOK])
        logits_lo = sb("logits_lo", [P, TP, E])
        logits = sb("logits", [P, TP, E])
        top = sb("top", [P, TP, 8])
        top_no = sb("top_no", [P, TP, 8], mybir.dt.uint32)
        top_id = sb("top_id", [P, TP, 2])
        gap = sb("gap", [P, TP])
        e_gap = sb("e_gap", [P, TP])
        one_e = sb("one_e", [P, TP])
        inv_e = sb("inv_e", [P, TP])
        w_top = sb("w_top", [P, TP, 2])
        is_top = sb("is_top", [P, 2, TP, E])
        w_is_top = sb("w_is_top", [P, 2, TP, E])
        scores = sb("scores", [P, TP, E])
        scoresT = sb("scoresT", [E, TOK])
        score_row = sb("score_row", [1, PAIRS, E, TOK])
        score_bc = sb("score_bc", [P, 2, TOK])
        tanh_g = sb("tanh_g", [P, 2, TOK])
        scaled = sb("scaled", [P, TOK])
        gated = sb("gated", [P, TOK])
        h = sb("h", [P, 2, TOK])
        h_hi = sb("h_hi", [P, 2, TOK], f32r)
        h_lo = sb("h_lo", [P, 2, TOK], f32r)

        def bank(name, shape):
            return ctx.enter_context(nc.psum_tensor(name, shape, f32))

        ps_g = [bank(f"ps_g{i}", [P, TOK]) for i in range(2)]
        ps_u = [bank(f"ps_u{i}", [P, TOK]) for i in range(2)]
        ps_out = [bank(f"ps_out{i}", [P, 2 * N]) for i in range(2)]
        ps_a = [bank(f"ps_a{i}", [P, TOK]) for i in range(2)]

        x_in = [sem(f"x_in{b}") for b in range(3)]
        ctx_in = [sem(f"ctx_in{p}") for p in range(PAIRS)]
        wq_in = sem("wq_in")
        wk_in = sem("wk_in")
        warm_ready = sem("warm_ready")
        bias_in = sem("bias_in")
        gate_in = sem("gate_in")
        gu_in = [sem(f"gu_in{i}") for i in range(GU_LOADS)]
        down_in = [sem(f"down_in{i}") for i in range(2)]
        consts = sem("consts")
        att_filled = sem("att_filled")
        act_drained = sem("act_drained")
        dve_drained = sem("dve_drained")
        dve_step = sem("dve_step")
        var_ready = sem("var_ready")
        rstd_ready = sem("rstd_ready")
        ln_ready = [sem(f"ln_ready{p}") for p in range(PAIRS)]
        hs_ready = sem("hs_ready")
        max_ready = sem("max_ready")
        exp_ready = sem("exp_ready")
        neg_mr_ready = sem("neg_mr_ready")
        probs_ready = sem("probs_ready")
        hi_ready = sem("hi_ready")
        gap_ready = sem("gap_ready")
        egap_ready = sem("egap_ready")
        scores_ready = sem("scores_ready")
        row_ready = sem("row_ready")
        gu_hi_ready = sem("gu_hi_ready")
        gu_lo_ready = sem("gu_lo_ready")
        down_hi_ready = sem("down_hi_ready")
        down_lo_ready = sem("down_lo_ready")
        gu_filled = sem("gu_filled")
        tanh_ready = sem("tanh_ready")
        bc_ready = sem("bc_ready")
        scaled_ready = sem("scaled_ready")
        gated_ready = sem("gated_ready")
        h_ready = sem("h_ready")
        h_hi_ready = sem("h_hi_ready")
        h_lo_ready = sem("h_lo_ready")
        last_lo_ready = sem("last_lo_ready")
        down_done = sem("down_done")
        out_ps0_ready = sem("out_ps0_ready")
        out_ready = sem("out_ready")
        stored = [sem(f"stored{b}") for b in range(B)]

        BANKS = [ps_out[0], ps_g[0], ps_u[0], ps_g[1], ps_u[1], ps_out[1], ps_a[0], ps_a[1]]
        FILLS = [(0, "ctxT0"), (0, "wq"), (0, "ctxT1"), (0, "wk"), (0, "q0"), (0, "k0"), (0, "q1"), (0, "k1"),
                 (0, "E0"), (0, "E1"), (1, "ctxT"), (1, "q"), (0, "LT0"), (0, "AT0"), (0, "LT1"),
                 (0, "AT1"), (0, "gateT"), (0, "M0"), (0, "M1"), (1, "k"), (1, "LT0"), (1, "LT1"), (0, "H0"), (0, "H1"),
                 (1, "E0"), (0, "logitsT"), (0, "logits"), (1, "E1"), (0, "scoresT"), (1, "AT0"), (1, "AT1"),
                 (1, "M0"), (1, "M1"), (1, "H0"), (1, "H1"), (1, "logitsT"), (1, "logits"), (1, "scoresT")]
        BEFORE_EXPERTS = FILLS.index((0, "logitsT"))
        ACT_READS = [(0, "ctxT0"), (0, "ctxT1"), (0, "q0"), (0, "q1"), (0, "k1"), (1, "ctxT"), (0, "E0"),
                     (0, "E1"), (0, "LT0"), (0, "AT0"), (1, "q"), (0, "LT1"), (0, "AT1"), (1, "k"), (1, "LT0"),
                     (1, "LT1"), (0, "logitsT"), (1, "E0"), (0, "scoresT"), (1, "E1"), (1, "AT0"), (1, "AT1"),
                     (1, "logitsT"), (1, "scoresT")]
        DVE_READS = [(0, "wq"), (0, "wk"), (0, "k0"), (0, "gateT"), (0, "M0"), (0, "M1"), (0, "H0"), (0, "H1"),
                     (0, "logits"), (1, "M0"), (1, "M1"), (1, "H0"), (1, "H1"), (1, "logits")]
        BANK = {}
        for use in FILLS:
            in_six = use[0] == 0 and use[1] not in ("wq", "wk", "gateT")
            turn = sum((b < 6) == in_six for b in BANK.values())
            BANK[use] = turn % 6 if in_six else 6 + turn % 2

        def bank_of(p, name):
            return BANKS[BANK[p, name]]

        def filled(p, name):
            return FILLS.index((p, name)) + 1

        def drain_count(p, name):
            reads = DVE_READS if (p, name) in DVE_READS else ACT_READS
            return reads.index((p, name)) + 1

        def wait_drained(eng, p, name):
            eng.wait_ge(dve_drained if (p, name) in DVE_READS else act_drained, drain_count(p, name))

        def wait_bank_free(eng, p, name):
            before = [u for u in FILLS[:filled(p, name) - 1] if BANK[u] == BANK[p, name]]
            if before:
                wait_drained(eng, *before[-1])

        WOVEN = {1: ([(1, "AT1"), (1, "M0"), (1, "M1")], []), 4: ([(1, "H0"), (1, "H1")], [])}
        INSERTED = {(0, 0): (0, "logitsT hi"), (0, 2): (0, "logitsT"), (0, 5): (0, "logits"), (0, 7): (1, "E1"),
                    (1, 5): (0, "scoresT"), (1, 10): (1, "AT0"),
                    (6, 0): (1, "logitsT hi"), (6, 2): (1, "logitsT"), (6, 6): (1, "logits"),
                    (7, 6): (1, "scoresT")}

        def batch(name):
            return int(name[-1])

        def pair_cols(name):
            return slice(batch(name) * N, (batch(name) + 1) * N) if name[-1].isdigit() else slice(0, 2 * N)

        def gu_src(e):
            return gu_raw[:, e].rearrange("p k (i two) -> p k two i", two=2)

        HALVES = [slice(0, L), slice(L, TOK)]

        block = ctx.enter_context(nc.Block())

        @block.sync
        def _(sp):
            def load_gu(i):
                es = slice(i * EL, (i + 1) * EL)
                sp.dma_start(gu_raw[:, es], gate_up[es].rearrange("e (k q) f -> q e k f", q=P)).then_inc(gu_in[i], 16)

            def load_rows(dst, src, p, done):
                sp.dma_start(dst[:, p * TP:(p + 1) * TP, :],
                             src[2 * p:2 * p + 2].rearrange("b (t q) n -> q (b t) n", q=P)).then_inc(done, 16)

            def load_down(i):
                es = slice(i * E // 2, (i + 1) * E // 2)
                sp.dma_start(down_raw[:, es], down[es].rearrange("e i n -> i e n")).then_inc(down_in[i], 16)

            load_rows(ctx_sb, ctx_feats, 0, ctx_in[0])
            sp.dma_start(wqk_sb[:, 1], Wk).then_inc(wk_in, 16)
            sp.dma_start(bias_sb[:, 0:1], bq.rearrange("(d o) -> d o", o=1)).then_inc(bias_in, 16)
            sp.dma_start(bias_sb[:, 1:2], bk.rearrange("(d o) -> d o", o=1)).then_inc(bias_in, 16)
            sp.dma_start(x_sb[:, LT:2 * LT, :], x[1].rearrange("(t q) n -> q t n", q=P)).then_inc(x_in[1], 16)
            sp.dma_start(gate_sb[:], router_gate).then_inc(gate_in, 16)
            load_rows(ctx_sb, ctx_feats, 1, ctx_in[1])
            load_gu(0)
            load_rows(x_sb, x, 1, x_in[2])
            load_gu(1)
            load_down(0)
            load_gu(2)
            load_gu(3)
            load_down(1)
            for p in range(PAIRS):
                wait_drained(sp, p, "scoresT")
                sp.dma_start(score_row[0:1, p], scoresT[:]).then_inc(row_ready, 16)
            for b in range(B):
                sp.wait_ge(out_ready, b + 1)
                sp.dma_start(out[b].rearrange("(t q) n -> q t n", q=P),
                             x1_sb[:, b * LT:(b + 1) * LT, :]).then_inc(stored[b], 16)
            for b in range(B):
                sp.wait_ge(stored[b], 16)

        @block.gpsimd
        def _(pool):
            nc.gpsimd.memset(ident[:], 0.0).then_inc(consts, 1)
            nc.gpsimd.memset(minus_half[:], -0.5).then_inc(consts, 1)
            pool.wait_ge(consts, 1)
            nc.gpsimd.affine_select(out=ident[:], in_=ident[:], compare_op=ALU.not_equal, fill=1.0, base=0,
                                    pattern=[[-1, P]], channel_multiplier=1).then_inc(consts, 1)
            nc.gpsimd.iota(expert_no[:], pattern=[[0, TP], [1, E]], base=0, channel_multiplier=0).then_inc(consts, 1)

            def inv_sqrt(n, src, dst, t0, t1):
                pool.wait_ge(var_ready, n)
                nc.gpsimd.tensor_tensor(dst[:, t0:t1], src[:, t0:t1], minus_half[:, t0:t1],
                                        ALU.pow).then_inc(rstd_ready, 1)

            def gu_lo_part(e):
                pool.wait_ge(gu_hi_ready, e + 1)
                nc.gpsimd.tensor_tensor(gu_lo[:, e], gu_src(e), gu_hi[:, e].bitcast(f32),
                                        ALU.subtract).then_inc(gu_lo_ready, 1)

            def down_lo_part(e):
                pool.wait_ge(down_hi_ready, e + 1)
                nc.gpsimd.tensor_tensor(down_lo[:, e], down_raw[:, e], down_hi[:, e].bitcast(f32),
                                        ALU.subtract).then_inc(down_lo_ready, 1)

            def broadcast(U):
                p, e = divmod(U, E)
                if e == 0:
                    pool.wait_ge(row_ready, 16 * (p + 1))
                if U >= 2:
                    pool.wait_ge(scaled_ready, U - 1)
                nc.gpsimd.partition_broadcast(score_bc[:, U % 2], score_row[0:1, p, e], P).then_inc(bc_ready, 1)

            inv_sqrt(1, var_eps, rstd, 0, LT)
            inv_sqrt(2, var_eps, rstd, LT, TP)
            inv_sqrt(3, var_eps, rstd, 0, TP)
            gu_lo_part(0)
            inv_sqrt(4, var_eps2, rstd2, 0, LT)
            inv_sqrt(5, var_eps2, rstd2, LT, TP)
            gu_lo_part(1)
            gu_lo_part(2)
            down_lo_part(0)
            broadcast(0)
            for U in range(UNITS):
                if U + 1 < UNITS:
                    broadcast(U + 1)
                if U == 0:
                    gu_lo_part(3)
                if U == 1:
                    inv_sqrt(6, var_eps2, rstd2, 0, LT)
                if U == 2:
                    inv_sqrt(7, var_eps2, rstd2, LT, TP)
                if U == UNITS - 1:
                    break
                pool.wait_ge(h_hi_ready, U + 1)
                if U >= 2:
                    pool.wait_ge(down_done, U - 1)
                nc.gpsimd.tensor_tensor(h_lo[:, U % 2], h[:, U % 2], h_hi[:, U % 2].bitcast(f32),
                                        ALU.subtract).then_inc(h_lo_ready, 1)
                if U + 1 < E:
                    down_lo_part(U + 1)
                if U + 4 < E:
                    gu_lo_part(U + 4)

        @block.tensor
        def _(pe):
            def att(p, name):
                wait_bank_free(pe, p, name.split()[0])
                dst = bank_of(p, name.split()[0])
                if name[:4] == "ctxT":
                    pe.wait_ge(ctx_in[p], 16)
                    t0 = pair_cols(name).start // P
                    for j in range(t0, pair_cols(name).stop // P):
                        last = nc.tensor.transpose(dst[:, (j - t0) * P:(j - t0 + 1) * P], ctx_sb[:, p * TP + j],
                                                   ident[:])
                elif name in ("wq", "wk"):
                    pe.wait_ge(wq_in if name == "wq" else wk_in, 16)
                    last = nc.tensor.transpose(dst[:, 0:P], wqk_sb[:, "qk".index(name[1])], ident[:])
                elif name == "gateT":
                    pe.wait_ge(gate_in, 16)
                    for c in range(NT):
                        last = nc.tensor.transpose(dst[:, c * E:(c + 1) * E], gate_sb[:, c * P:(c + 1) * P],
                                                   ident[0:E, 0:E])
                elif name[0] in "qk":
                    wait_drained(pe, 0, "w" + name[0])
                    wait_drained(pe, p, "ctxT" + name[1:])
                    cols = pair_cols(name)
                    last = nc.tensor.matmul(dst[:, 0:cols.stop - cols.start], wqkT[:, "qk".index(name[0])],
                                            ctxT[:, cols], start=True, stop=True)
                elif name[0] == "E":
                    digit = name[1] if p == 0 else ""
                    wait_drained(pe, p, "q" + digit)
                    wait_drained(pe, p, "k" + digit)
                    o = batch(name) * N
                    for t in range(NT):
                        last = nc.tensor.matmul(dst[:, t * N:(t + 1) * N], qT[:, o + t * P:o + (t + 1) * P],
                                                kT[:, o:o + N], start=True, stop=True)
                elif name[:2] in ("LT", "AT"):
                    bi = int(name[2])
                    if name[0] == "L":
                        src = ln
                        pe.wait_ge(ln_ready[p], (bi + 1) * LT)
                    else:
                        src = probs
                        pe.wait_ge(probs_ready, 2 * p + bi + 1)
                    v = dst[:].rearrange("q (k r) -> q k r", k=NT)
                    for t in range(2):
                        for c in range(NT):
                            last = nc.tensor.transpose(v[:, c, t * P:(t + 1) * P],
                                                       src[:, bi * LT + t, c * P:(c + 1) * P], ident[:])
                elif name[0] == "M":
                    bi = int(name[1])
                    wait_drained(pe, p, f"LT{bi}")
                    wait_drained(pe, p, f"AT{bi}")
                    for t in range(LT):
                        for c in range(NT):
                            last = nc.tensor.matmul(dst[:, t * N:(t + 1) * N], lnT[:, bi, c, t * P:(t + 1) * P],
                                                    probsT[:, bi, c], start=(c == 0), stop=(c == NT - 1))
                elif name[0] == "H":
                    bi = int(name[1])
                    pe.wait_ge(hs_ready, p * TP + (bi + 1) * LT)
                    v = dst[:].rearrange("q (k r) -> q k r", k=NT)
                    for t in range(LT):
                        for c in range(NT):
                            last = nc.tensor.transpose(v[:, c, t * P:(t + 1) * P],
                                                       hs[:, bi * LT + t, c * P:(c + 1) * P], ident[:])
                elif name[:7] == "logitsT":
                    lo_part = name == "logitsT"
                    if lo_part:
                        wait_drained(pe, p, "H1")
                    else:
                        pe.wait_ge(hi_ready, 2 * (p + 1))
                        wait_drained(pe, 0, "gateT")
                    for c in range(NT):
                        last = nc.tensor.matmul(dst[0:2 * E, :], gateT[:, c].rearrange("q s e -> q (s e)"),
                                                (hsT_lo if lo_part else hsT_hi)[:, p, c],
                                                start=(not lo_part and c == 0), stop=(lo_part and c == NT - 1))
                    if not lo_part:
                        return
                elif name == "logits":
                    wait_drained(pe, p, "logitsT")
                    for j in range(TP):
                        last = nc.tensor.transpose(dst[:, j * 2 * E:(j + 1) * 2 * E], logitsT[:, j * P:(j + 1) * P],
                                                   ident[0:2 * E, 0:2 * E])
                else:
                    pe.wait_ge(scores_ready, p + 1)
                    for j in range(TP):
                        last = nc.tensor.transpose(dst[0:E, j * P:(j + 1) * P], scores[:, j], ident[:])
                last.then_inc(att_filled, 1)

            pe.wait_ge(warm_ready, 1)
            for _ in range(WARM_UP):
                nc.tensor.matmul(ps_out[0][:, 0:P], warm[:], warm[:], start=True, stop=True)
            pe.wait_ge(consts, 4)
            for p, name in FILLS[:BEFORE_EXPERTS]:
                att(p, name)

            def gate_up_unit(U):
                p, e = divmod(U, E)
                if e == 0:
                    pe.wait_ge(hi_ready, 2 * (p + 1))
                if p == 0:
                    pe.wait_ge(gu_lo_ready, e + 1)
                if U >= 2:
                    pe.wait_ge(h_ready, U - 1)
                if U == 1:
                    wait_drained(pe, 0, "logitsT")
                terms = [(w, a, c) for w, a in ((gu_lo, hsT_hi), (gu_hi, hsT_hi), (gu_hi, hsT_lo)) for c in range(NT)]
                for half, dst in enumerate((ps_g[U % 2], ps_u[U % 2])):
                    for i, (w, a, c) in enumerate(terms):
                        if (U, half * len(terms) + i) in INSERTED:
                            att(*INSERTED[U, half * len(terms) + i])
                        if e == 0 and half == 0 and i == 2 * NT:
                            wait_drained(pe, p, "H1")
                        last = nc.tensor.matmul(dst[:], w[:, e, c, half], a[:, p, c],
                                                start=(i == 0), stop=(i == len(terms) - 1))
                        if i == len(terms) - 1:
                            last.then_inc(gu_filled, 1)

            def down_unit(U):
                p, e = divmod(U, E)
                if U < UNITS - 1:
                    pe.wait_ge(h_lo_ready, U + 1)
                if p == 0:
                    pe.wait_ge(down_lo_ready, e + 1)
                if U == 0:
                    wait_drained(pe, 0, "logits")
                    wait_drained(pe, 0, "scoresT")
                if e == 0 and p > 0:
                    pe.wait_ge(out_ready, 2 * p)
                for j in range(TP):
                    if U == UNITS - 1 and j % 2 == 0:
                        pe.wait_ge(last_lo_ready, j // 2 + 1)
                    cols = slice(j * P, (j + 1) * P)
                    dst = ps_out[j // 2][:, (j % 2) * N:(j % 2 + 1) * N]
                    terms = ((h_lo, down_hi), (h_hi, down_lo), (h_hi, down_hi))
                    for i, (a, w) in enumerate(terms):
                        last = nc.tensor.matmul(dst, a[:, U % 2, cols], w[:, e],
                                                start=(e == 0 and i == 0 and j % 2 == 0),
                                                stop=(e == E - 1 and i == 2), skip_group_check=True)
                    if j == TP - 1:
                        last.then_inc(down_done, 1)
                    elif e == E - 1 and j % 2 == 1:
                        last.then_inc(out_ps0_ready, 1)

            for U in range(UNITS + 2):
                before_down, after_down = WOVEN.get(U, ([], []))
                if U < UNITS:
                    gate_up_unit(U)
                for p, name in before_down:
                    att(p, name)
                if U >= 2:
                    down_unit(U - 2)
                for p, name in after_down:
                    att(p, name)

        @block.scalar
        def _(act):
            act.dma_start(wqk_sb[:, 0], Wq).then_inc(wq_in, 16)
            act.dma_start(x_sb[:, 0:LT, :], x[0].rearrange("(t q) n -> q t n", q=P)).then_inc(x_in[0], 16)
            nc.scalar.preload_act_table(ACT.Exp)

            def split_gu(e):
                if e % EL == 0:
                    act.wait_ge(gu_in[e // EL], 16)
                nc.scalar.copy(gu_hi[:, e], gu_src(e)).then_inc(gu_hi_ready, 1)

            def att(p, name):
                src = bank_of(p, name)
                if name[:4] == "ctxT":
                    act.wait_ge(att_filled, filled(p, name))
                    cols = pair_cols(name)
                    nc.scalar.copy(ctxT[:, cols], src[:, 0:cols.stop - cols.start]).then_inc(act_drained, 1)
                elif name[0] in "qk":
                    act.wait_ge(att_filled, filled(p, name))
                    act.wait_ge(bias_in, 16 * 2)
                    i, cols = "qk".index(name[0]), pair_cols(name)
                    nc.scalar.activation((qT, kT)[i][:, cols], src[:, 0:cols.stop - cols.start], ACT.Identity,
                                         bias=bias_sb[:, i:i + 1]).then_inc(act_drained, 1)
                elif name[:2] in ("LT", "AT"):
                    act.wait_ge(att_filled, filled(p, name))
                    nc.scalar.copy((lnT if name[0] == "L" else probsT)[:, batch(name)].rearrange("q k r -> q (k r)"),
                                   src[:]).then_inc(act_drained, 1)
                elif name in ("E0", "E1"):
                    bi = int(name[1])
                    act.wait_ge(max_ready, 2 * p + bi + 1)
                    for t in range(2):
                        j = 2 * bi + t
                        nc.scalar.activation(probs[:, j], src[:, t * N:(t + 1) * N], ACT.Exp,
                                             bias=neg_max[:, j:j + 1],
                                             accum_out=denom[:, j:j + 1]).then_inc(exp_ready, 1)
                    act.wait_ge(exp_ready, 4 * p + 2 * bi + 2)
                    act.sem_inc(act_drained, 1)
                elif name in ("H0", "H1"):
                    bi = int(name[1])
                    act.wait_ge(att_filled, filled(p, name))
                    v = bank_of(p, name)[:].rearrange("q (k r) -> q k r", k=NT)
                    nc.scalar.copy(hsT_hi[:, p, :, bi * L:(bi + 1) * L], v).then_inc(hi_ready, 1)
                elif name == "logitsT":
                    act.wait_ge(att_filled, filled(p, name))
                    nc.scalar.copy(logitsT[:], src[0:2 * E, :]).then_inc(act_drained, 1)
                elif name == "logits":
                    act.wait_ge(gap_ready, p + 1)
                    nc.scalar.activation(e_gap[:], gap[:], ACT.Exp).then_inc(egap_ready, 1)
                elif name == "scoresT":
                    act.wait_ge(att_filled, filled(p, name))
                    if p > 0:
                        act.wait_ge(row_ready, 16 * p)
                    nc.scalar.copy(scoresT[:], bank_of(p, name)[0:E, :]).then_inc(act_drained, 1)

            def ln_pair_1():
                act.wait_ge(neg_mr_ready, 1)
                act.wait_ge(att_filled, filled(0, "LT1"))
                for j in range(TP):
                    nc.scalar.activation(ln[:, j], x_sb[:, TP + j], ACT.Identity, bias=neg_mr[:, j:j + 1],
                                         scale=rstd[:, j:j + 1]).then_inc(ln_ready[1], 1)

            for p, name in ACT_READS[:ACT_READS.index((1, "k"))]:
                att(p, name)
            split_gu(0)
            split_gu(1)
            ln_pair_1()
            for p, name in ((1, "k"), (1, "LT0"), (1, "LT1"), (0, "H0"), (0, "H1")):
                att(p, name)
            split_gu(2)
            for p, name in ((0, "logitsT"), (1, "E0"), (0, "logits")):
                att(p, name)
            def split_h(U):
                if U >= 2:
                    act.wait_ge(down_done, U - 1)
                for i, part in enumerate([slice(0, TOK)] if U < UNITS - 1 else HALVES):
                    act.wait_ge(h_ready, U + 1 + i)
                    nc.scalar.copy(h_hi[:, U % 2, part], h[:, U % 2, part]).then_inc(h_hi_ready, 1)

            for U in range(UNITS):
                act.wait_ge(gu_filled, 2 * U + 1)
                if U >= 2:
                    act.wait_ge(scaled_ready, U - 1)
                for part in [slice(0, TOK)] if U < UNITS - 1 else HALVES:
                    nc.scalar.activation(tanh_g[:, U % 2, part], ps_g[U % 2][:, part], ACT.Tanh,
                                         scale=0.5).then_inc(tanh_ready, 1)
                if U >= 1:
                    split_h(U - 1)
                if U == 0:
                    att(0, "scoresT")
                    att(1, "E1")
                    att(1, "AT0")
                    att(1, "AT1")
                    split_gu(3)
                if U in (1, 2):
                    split_gu(2 * U + 2)
                    split_gu(2 * U + 3)
                if U == 4:
                    att(1, "H0")
                    att(1, "H1")
                if U == 5:
                    att(1, "logitsT")
                if U == 6:
                    att(1, "logits")
                    att(1, "scoresT")
            split_h(UNITS - 1)

        @block.vector
        def _(dve):
            steps = [0]

            def step(ins):
                ins.then_inc(dve_step, 1)
                steps[0] += 1
                dve.wait_ge(dve_step, steps[0])

            def mean_and_var(src, tiles, st, mv, ve):
                for i, j in enumerate(tiles):
                    ins = nc.vector.bn_stats(st[:, j], src(j))
                    ins.then_inc(dve_step, 1)
                    steps[0] += 1
                dve.wait_ge(dve_step, steps[0])
                for j in tiles:
                    ins = nc.vector.bn_aggr(mv[:, j], st[:, j])
                    ins.then_inc(dve_step, 1)
                    steps[0] += 1
                dve.wait_ge(dve_step, steps[0])
                t = slice(tiles[0], tiles[-1] + 1)
                nc.vector.tensor_scalar_add(ve[:, t], mv[:, t, 1], EPS).then_inc(var_ready, 1)

            def normalise(n, src, tiles, mv, rs, dst, ready):
                dve.wait_ge(rstd_ready, n)
                for j in tiles:
                    nc.vector.tensor_scalar(dst[:, j], src(j), mv[:, j, 0:1], rs[:, j:j + 1],
                                            ALU.subtract, ALU.mult).then_inc(ready, 1)

            def att(p, name):
                def x1t(j):
                    return x1_sb[:, p * TP + j]

                if name in ("wq", "wk"):
                    dve.wait_ge(att_filled, filled(p, name))
                    nc.vector.tensor_copy(wqkT[:, "qk".index(name[1])], bank_of(p, name)[:, 0:P]).then_inc(dve_drained, 1)
                elif name == "k0":
                    dve.wait_ge(att_filled, filled(p, name))
                    dve.wait_ge(bias_in, 16 * 2)
                    nc.vector.tensor_scalar(kT[:, 0:N], bank_of(p, name)[:, 0:N], bias_sb[:, 1:2], None,
                                            ALU.add).then_inc(dve_drained, 1)
                elif name == "gateT":
                    dve.wait_ge(att_filled, filled(p, name))
                    gate_ps = bank_of(p, name)[:, 0:NT * E].rearrange("q (c e) -> q c e", c=NT)
                    step(nc.vector.tensor_copy(gateT[:, :, 0], gate_ps))
                    nc.vector.tensor_tensor(gateT[:, :, 1], gate_ps, gateT[:, :, 0].bitcast(f32),
                                            ALU.subtract).then_inc(dve_drained, 1)
                elif name in ("E0", "E1"):
                    bi = int(name[1])
                    dve.wait_ge(att_filled, filled(p, name))
                    nc.vector.tensor_reduce(neg_max[:, 2 * bi:2 * bi + 2],
                                            bank_of(p, name)[:].rearrange("q (t n) -> q t n", t=2),
                                            AX.X, ALU.max, negate=True).then_inc(max_ready, 1)
                elif name in ("AT0", "AT1"):
                    bi = int(name[2])
                    dve.wait_ge(exp_ready, 4 * p + 2 * bi + 2)
                    step(nc.vector.reciprocal(rdenom[:, 2 * bi:2 * bi + 2], denom[:, 2 * bi:2 * bi + 2]))
                    for t in range(2):
                        j = 2 * bi + t
                        last = nc.vector.tensor_scalar(probs[:, j], probs[:, j], rdenom[:, j:j + 1], None, ALU.mult)
                    last.then_inc(probs_ready, 1)
                elif name in ("M0", "M1"):
                    bi = int(name[1])
                    t0 = p * TP + bi * LT
                    dve.wait_ge(att_filled, filled(p, name))
                    ins = nc.vector.tensor_tensor(x1_sb[:, t0:t0 + LT].rearrange("q t n -> q (t n)"),
                                                  bank_of(p, name)[:],
                                                  x_sb[:, t0:t0 + LT].rearrange("q t n -> q (t n)"), ALU.add)
                    ins.then_inc(dve_drained, 1)
                    if (p, bi) == (0, 0):
                        dve.wait_ge(rstd_ready, 3)
                        nc.vector.scalar_tensor_tensor(out=neg_mr[:], in0=mean_var[:, :, 0], scalar=-1.0, in1=rstd[:],
                                                       op0=ALU.mult, op1=ALU.mult).then_inc(neg_mr_ready, 1)
                    dve.wait_ge(dve_drained, drain_count(p, name))
                    mean_and_var(x1t, [bi * LT, bi * LT + 1], stats2, mean_var2, var_eps2)
                elif name in ("H0", "H1"):
                    bi = int(name[1])
                    dve.wait_ge(hi_ready, 2 * p + bi + 1)
                    v = bank_of(p, name)[:].rearrange("q (k r) -> q k r", k=NT)
                    cols = slice(bi * L, (bi + 1) * L)
                    nc.vector.tensor_tensor(hsT_lo[:, p, :, cols], v, hsT_hi[:, p, :, cols].bitcast(f32),
                                            ALU.subtract).then_inc(dve_drained, 1)
                elif name == "logits":
                    route(p)

            def norm_x1(p, bi):
                normalise(2 * p + 4 + bi, lambda j: x1_sb[:, p * TP + j], [bi * LT, bi * LT + 1],
                          mean_var2, rstd2, hs, hs_ready)

            def route(p):
                dve.wait_ge(att_filled, filled(p, "logits"))
                parts = bank_of(p, "logits")[:, 0:TP * 2 * E].rearrange("q (t s e) -> q t s e", t=TP, s=2)
                step(nc.vector.tensor_copy(logits_lo[:], parts[:, :, 1]))
                nc.vector.tensor_tensor(logits[:], parts[:, :, 0], logits_lo[:], ALU.add).then_inc(dve_drained, 1)
                dve.wait_ge(dve_drained, drain_count(p, "logits"))
                for j in range(TP):
                    ins = nc.vector.max(top[:, j], logits[:, j])
                    ins.then_inc(dve_step, 1)
                    steps[0] += 1
                dve.wait_ge(dve_step, steps[0])
                nc.vector.tensor_tensor(gap[:], top[:, :, 1], top[:, :, 0], ALU.subtract).then_inc(gap_ready, 1)
                for j in range(TP):
                    ins = nc.vector.max_index(top_no[:, j], top[:, j], logits[:, j])
                    ins.then_inc(dve_step, 1)
                    steps[0] += 1
                dve.wait_ge(dve_step, steps[0])
                step(nc.vector.tensor_copy(top_id[:], top_no[:, :, 0:2]))
                for r in range(2):
                    ins = nc.vector.tensor_tensor(is_top[:, r], expert_id[:],
                                                  top_id[:, :, r:r + 1].broadcast_to([P, TP, E]), ALU.is_equal)
                    ins.then_inc(dve_step, 1)
                    steps[0] += 1
                dve.wait_ge(egap_ready, p + 1)
                step(nc.vector.tensor_scalar(one_e[:], e_gap[:], 1.0, 2.0, ALU.add, ALU.mult))
                step(nc.vector.reciprocal(w_top[:, :, 0], one_e[:]))
                step(nc.vector.tensor_tensor(w_top[:, :, 1], w_top[:, :, 0], e_gap[:], ALU.mult))
                for r in range(2):
                    ins = nc.vector.tensor_tensor(w_is_top[:, r], is_top[:, r],
                                                  w_top[:, :, r:r + 1].broadcast_to([P, TP, E]), ALU.mult)
                    ins.then_inc(dve_step, 1)
                    steps[0] += 1
                dve.wait_ge(dve_step, steps[0])
                nc.vector.tensor_tensor(scores[:], w_is_top[:, 0], w_is_top[:, 1], ALU.add).then_inc(scores_ready, 1)

            def split_down(e):
                if e % (E // 2) == 0:
                    dve.wait_ge(down_in[e // (E // 2)], 16)
                nc.vector.tensor_copy(down_hi[:, e], down_raw[:, e]).then_inc(down_hi_ready, 1)

            def xt(j):
                return x_sb[:, j]

            nc.vector.memset(warm[:], 0.0).then_inc(warm_ready, 1)
            dve.wait_ge(consts, 4)
            step(nc.vector.tensor_copy(expert_id[:], expert_no[:]))
            for name in ("wq", "wk", "k0"):
                att(0, name)
            for bi in range(2):
                dve.wait_ge(x_in[bi], 16)
                mean_and_var(xt, [bi * LT, bi * LT + 1], stats, mean_var, var_eps)
            att(0, "E0")
            normalise(1, xt, [0, 1], mean_var, rstd, ln, ln_ready[0])
            att(0, "E1")
            att(0, "AT0")
            normalise(2, xt, [2, 3], mean_var, rstd, ln, ln_ready[0])
            att(0, "AT1")
            dve.wait_ge(ln_ready[0], TP)
            dve.wait_ge(x_in[2], 16)
            mean_and_var(lambda j: x_sb[:, TP + j], list(range(TP)), stats, mean_var, var_eps)
            att(0, "gateT")
            att(0, "M0")
            att(0, "M1")
            norm_x1(0, 0)
            norm_x1(0, 1)
            att(0, "H0")
            att(0, "H1")
            att(1, "E0")
            for e in range(E // 2):
                split_down(e)
            att(0, "logits")
            att(1, "E1")
            att(1, "AT0")
            att(1, "AT1")
            for e in range(E // 2, E):
                split_down(e)

            def finish(p, i):
                t0 = p * TP + i * LT
                if i == 0:
                    dve.wait_ge(out_ps0_ready, p + 1)
                else:
                    dve.wait_ge(down_done, (p + 1) * E)
                nc.vector.tensor_tensor(x1_sb[:, t0:t0 + LT], ps_out[i][:].rearrange("q (t n) -> q t n", t=LT), x1_sb[:, t0:t0 + LT],
                                        ALU.add).then_inc(out_ready, 1)

            for U in range(UNITS):
                parts = [slice(0, TOK)] if U < UNITS - 1 else HALVES
                dve.wait_ge(bc_ready, U + 1)
                for i, part in enumerate(parts):
                    dve.wait_ge(tanh_ready, U + 1 + i)
                    nc.vector.scalar_tensor_tensor(out=scaled[:, part], in0=tanh_g[:, U % 2, part], scalar=1.0,
                                                   in1=score_bc[:, U % 2, part], op0=ALU.add,
                                                   op1=ALU.mult).then_inc(scaled_ready, 1)
                for i, part in enumerate(parts):
                    dve.wait_ge(tanh_ready, U + len(parts))
                    dve.wait_ge(scaled_ready, U + 1 + i)
                    nc.vector.tensor_tensor(gated[:, part], ps_g[U % 2][:, part], scaled[:, part],
                                            ALU.mult).then_inc(gated_ready, 1)
                dve.wait_ge(gu_filled, 2 * U + 2)
                if U >= 2:
                    dve.wait_ge(h_lo_ready, U - 1)
                for i, part in enumerate(parts):
                    dve.wait_ge(gated_ready, U + 1 + i)
                    nc.vector.tensor_tensor(h[:, U % 2, part], ps_u[U % 2][:, part], gated[:, part],
                                            ALU.mult).then_inc(h_ready, 1)
                if U == UNITS - 1:
                    dve.wait_ge(down_done, U - 1)
                    for i, part in enumerate(parts):
                        dve.wait_ge(h_hi_ready, U + 1 + i)
                        nc.vector.tensor_tensor(h_lo[:, U % 2, part], h[:, U % 2, part],
                                                h_hi[:, U % 2, part].bitcast(f32),
                                                ALU.subtract).then_inc(last_lo_ready, 1)
                if U == 0:
                    att(1, "M0")
                if U == 1:
                    att(1, "M1")
                if U == 2:
                    norm_x1(1, 0)
                    norm_x1(1, 1)
                if U == 4:
                    att(1, "H0")
                    att(1, "H1")
                if U == 5:
                    att(1, "logits")
                if U == E + 1:
                    finish(0, 0)
                    finish(0, 1)
            finish(1, 0)
            finish(1, 1)


_INS = ['x', 'ctx_1024', 'L0_xattn_Wq', 'L0_xattn_bq', 'L0_xattn_Wk', 'L0_xattn_bk',
        'L0_ffn_router_gate', 'L0_ffn_expert_gate_up', 'L0_ffn_expert_down']
_OUTS = [((4, 256, 256), 'float32')]


def kernel(**inputs):
    import numpy as _np
    import concourse.bacc as _bacc
    from concourse import mybir as _mybir
    from concourse.bass_utils import run_bass_kernel_spmd as _run

    nc = _bacc.Bacc("TRN2", target_bir_lowering=False, num_devices=1)
    arrays, args = {}, []
    for name in _INS:
        a = _np.ascontiguousarray(inputs[name])
        arrays[f"in_{name}_dram"] = a
        args.append(nc.dram_tensor(f"in_{name}_dram", a.shape, _mybir.dt.from_np(a.dtype), kind="ExternalInput").ap())
    for i, (shape, dtype) in enumerate(_OUTS):
        dt = _mybir.dt.from_np(_np.dtype(dtype))
        args.append(nc.dram_tensor(f"out_{i}_dram", shape, dt, kind="ExternalOutput").ap())
    cross_attention_moe_kernel(nc, *args)
    r = _run(nc, [arrays], core_ids=[0])
    got = tuple(r.results[0][f"out_{i}_dram"] for i in range(len(_OUTS)))
    return got[0]
```
